# Optimizing a Trainium2 kernel written in Bass

```python
import numpy as np
import jax
import jax.numpy as jnp

def _softmax(x, axis=-1):
    return jax.nn.softmax(x, axis=axis)

def _gelu(x):
    return jax.nn.gelu(x, approximate=True)

def _silu(x):
    return jax.nn.silu(x)

def _sigmoid(x):
    return jax.nn.sigmoid(x)

def _layernorm(x, axis=-1, eps=1e-05):
    m = jnp.mean(x, axis=axis, keepdims=True)
    v = jnp.var(x, axis=axis, keepdims=True)
    return (x - m) / jnp.sqrt(v + eps)

def _scatter_add(tgt, idx, src, axis=0):
    return tgt.at[idx].add(src)

def _segment_sum(src, seg, n):
    return jax.ops.segment_sum(src, seg, n)
kernel_name = 'mk_seq_postln_d1_jaxref_r8_6379e1'

def setup_inputs(seed: int=0):
    np.random.seed(seed)
    _w = jnp.asarray

    def _L0_attn_setup():
        import jax, jax.numpy as jnp
        import numpy as np
        B, S, D_MODEL = (4, 256, 128)
        NUM_HEADS, HEAD_DIM = (16, 64)
        EPS = 1e-06
        key = jax.random.key(seed)
        ks = jax.random.split(key, 6)
        hd = NUM_HEADS * HEAD_DIM
        scale_in = 1.0 / np.sqrt(D_MODEL)
        scale_hd = 1.0 / np.sqrt(hd)
        return {'x': jax.random.normal(ks[0], (B, S, D_MODEL), dtype=jnp.float32), 'w_q': jax.random.normal(ks[1], (D_MODEL, hd), dtype=jnp.float32) * scale_in, 'w_k': jax.random.normal(ks[2], (D_MODEL, hd), dtype=jnp.float32) * scale_in, 'w_v': jax.random.normal(ks[3], (D_MODEL, hd), dtype=jnp.float32) * scale_in, 'w_proj': jax.random.normal(ks[4], (hd, D_MODEL), dtype=jnp.float32) * scale_hd, 'b_proj': jax.random.normal(ks[5], (D_MODEL,), dtype=jnp.float32) * 0.01, 'ln_gamma': jnp.ones((D_MODEL,), dtype=jnp.float32), 'ln_beta': jnp.zeros((D_MODEL,), dtype=jnp.float32)}
    _L0_attn_in = _L0_attn_setup()

    def _L0_ffn_setup():
        import jax, jax.numpy as jnp
        import numpy as np
        DIM = 128
        HIDDEN = 384
        SCALE = 1.0 / 127.0

        def _dequant(w_int, dtype):
            return w_int.astype(dtype) * jnp.asarray(SCALE, dtype)
        key = jax.random.key(seed)
        k_x, k_g, k_u, k_d = jax.random.split(key, 4)
        x = jax.random.normal(k_x, (4, 256, DIM), dtype=jnp.float32)
        w_gate = jax.random.randint(k_g, (HIDDEN, DIM), -127, 128, dtype=jnp.int32)
        w_up = jax.random.randint(k_u, (HIDDEN, DIM), -127, 128, dtype=jnp.int32)
        w_down = jax.random.randint(k_d, (DIM, HIDDEN), -127, 128, dtype=jnp.int32)
        return {'x': x, 'w_gate': w_gate, 'w_up': w_up, 'w_down': w_down}
    _L0_ffn_in = _L0_ffn_setup()
    _d = {'L0_attn_x': _L0_attn_in['x'], 'L0_attn_w_q': _L0_attn_in['w_q'], 'L0_attn_w_k': _L0_attn_in['w_k'], 'L0_attn_w_v': _L0_attn_in['w_v'], 'L0_attn_w_proj': _L0_attn_in['w_proj'], 'L0_attn_b_proj': _L0_attn_in['b_proj'], 'L0_attn_ln_gamma': _L0_attn_in['ln_gamma'], 'L0_attn_ln_beta': _L0_attn_in['ln_beta'], 'L0_ffn_w_gate': _L0_ffn_in['w_gate'], 'L0_ffn_w_up': _L0_ffn_in['w_up'], 'L0_ffn_w_down': _L0_ffn_in['w_down']}
    _x0 = _d['L0_attn_x']
    _d['L0_attn_x'] = jax.random.normal(jax.random.fold_in(jax.random.key(seed), 1), (4, 1024, 128), dtype=_x0.dtype)
    del _x0
    return _d

def reference(L0_attn_x, L0_attn_w_q, L0_attn_w_k, L0_attn_w_v, L0_attn_w_proj, L0_attn_b_proj, L0_attn_ln_gamma, L0_attn_ln_beta, L0_ffn_w_gate, L0_ffn_w_up, L0_ffn_w_down):

    def _L0_attn_ref(x, w_q, w_k, w_v, w_proj, b_proj, ln_gamma, ln_beta):
        import jax, jax.numpy as jnp
        import numpy as np
        B, S, D_MODEL = (4, 256, 128)
        NUM_HEADS, HEAD_DIM = (16, 64)
        EPS = 1e-06

        def split_heads(t):
            b, s, _ = t.shape
            return t.reshape(b, s, NUM_HEADS, HEAD_DIM).transpose(0, 2, 1, 3)
        q = split_heads(x @ w_q)
        k = split_heads(x @ w_k)
        v = split_heads(x @ w_v)
        scale = HEAD_DIM ** (-0.5)
        attn = jnp.einsum('bnqd,bnkd->bnqk', q, k) * scale
        attn = jax.nn.softmax(attn, axis=-1)
        o = jnp.einsum('bnqk,bnkd->bnqd', attn, v)
        o = o.transpose(0, 2, 1, 3).reshape(x.shape[0], x.shape[1], NUM_HEADS * HEAD_DIM)
        y = o @ w_proj + b_proj + x
        mean = jnp.mean(y, axis=-1, keepdims=True)
        var = jnp.var(y, axis=-1, keepdims=True)
        y = (y - mean) * jax.lax.rsqrt(var + EPS) * ln_gamma + ln_beta
        return y

    def _L0_ffn_ref(x, w_gate, w_up, w_down):
        import jax, jax.numpy as jnp
        import numpy as np
        DIM = 128
        HIDDEN = 384
        SCALE = 1.0 / 127.0

        def _dequant(w_int, dtype):
            return w_int.astype(dtype) * jnp.asarray(SCALE, dtype)
        wg = _dequant(w_gate, x.dtype)
        wu = _dequant(w_up, x.dtype)
        wd = _dequant(w_down, x.dtype)
        gate = jnp.einsum('bsd,hd->bsh', x, wg)
        up = jnp.einsum('bsd,hd->bsh', x, wu)
        h = jax.nn.silu(gate) * up
        return jnp.einsum('bsh,dh->bsd', h, wd)
    x = L0_attn_x
    x = _layernorm(x + _L0_attn_ref(x, L0_attn_w_q, L0_attn_w_k, L0_attn_w_v, L0_attn_w_proj, L0_attn_b_proj, L0_attn_ln_gamma, L0_attn_ln_beta), axis=-1)
    x = _layernorm(x + _L0_ffn_ref(x, L0_ffn_w_gate, L0_ffn_w_up, L0_ffn_w_down), axis=-1)
    return x

_drawn_inputs = setup_inputs


def setup_inputs(seed=0):
    import zlib

    import numpy as np

    out = dict(_drawn_inputs(seed))
    spreads = {'L0_attn_ln_gamma': (1.0, 0.2), 'L0_attn_ln_beta': (0.0, 0.1)}
    factors = {'L0_attn_b_proj': 6.191}
    for name, (base, spread) in spreads.items():
        noise = np.random.default_rng([zlib.crc32(name.encode()), seed]).standard_normal(out[name].shape)
        drawn = base * np.exp(spread * noise) if base else spread * noise
        out[name] = jnp.asarray(drawn.astype(out[name].dtype))
    for name, factor in factors.items():
        out[name] = (out[name] * factor).astype(out[name].dtype)
    return out
```

```python
from contextlib import ExitStack

import concourse.bass as bass
from concourse import mybir

F32 = mybir.dt.float32
F16 = mybir.dt.float16
I32 = mybir.dt.int32
ALU = mybir.AluOpType
ACT = mybir.ActivationFunctionType
AX_X = mybir.AxisListType.X

ROWS = (slice(0, 64), slice(64, 128))


def attention_ffn_program(nc, x, w_q, w_k, w_v, w_proj, b_proj, ln_gamma, ln_beta, w_gate, w_up, w_down, out):
    B, S, D = x.shape
    HD = w_q.shape[1]
    HIDDEN = w_gate.shape[0]
    DH = 64
    T = B * S
    TILES = T // 128
    KT = S // 128
    PB = HD // 128
    PAIRS = B * PB
    HB = HIDDEN // 128
    GROUP = 512
    GT = GROUP // 128
    GROUPS = T // GROUP
    RING = 4
    W_SCALE = 64.0
    Q_SCALE = DH ** -0.5 / W_SCALE
    MAXJ = 2 * KT * 2
    assert D == 128 and S == 1024 and DH * 2 == 128 and PB == 8

    with ExitStack() as ctx:
        def sb(name, shape, dt):
            return ctx.enter_context(nc.sbuf_tensor(name, shape, dt))

        def sem(name):
            return ctx.enter_context(nc.semaphore(name))

        x_tok = sb("x_tok", [128, T], F32)
        y_tok = sb("y_tok", [128, T], F32)
        x_split = sb("x_split", [128, B, 2, S], F16)
        w_split = sb("w_split", [128, PB, 6, 128], F16)
        wp_all = sb("wp_all", [128, PB, D], F32)
        x_slot = sb("x_slot", [128, 2, S], F16)
        w_slot = [sb(f"w_slot{s}", [128, 6, 128], F16) for s in range(2)]
        wp_slot = [sb(f"wp_slot{s}", [128, D], F32) for s in range(2)]
        q_hh = [[sb(f"q_hh{s}{h}", [128, S], F16) for h in range(2)] for s in range(2)]
        q_lm = [[sb(f"q_lm{s}{h}", [128, S], F16) for h in range(2)] for s in range(2)]
        k_hl = [[sb(f"k_hl{s}{h}", [128, S], F16) for h in range(2)] for s in range(2)]
        k_h1 = [[sb(f"k_h1{s}{h}", [128, S], F16) for h in range(2)] for s in range(2)]
        v_slot = [sb(f"v_slot{s}", [128, KT, 128], F32) for s in range(2)]
        probs = sb("probs", [128, RING, 2, S], F32)
        prob_sum = [sb(f"prob_sum{s}", [128, 2, S], F32) for s in range(2)]
        o_raw = [sb(f"o_raw{s}", [128, S], F32) for s in range(2)]
        o_norm = sb("o_norm", [128, S], F32)
        row_sum = sb("row_sum", [128, S], F32)
        row_inv = sb("row_inv", [128, S], F32)
        tile_max = sb("tile_max", [128, MAXJ // 2, 2], F32)
        max16 = sb("max16", [128, MAXJ // 2], F16)
        max_rows = sb("max_rows", [MAXJ // 2, 128], F16)
        ident = sb("ident", [128, 128], F32)
        neg_ident = sb("neg_ident", [128, 128], F16)
        ones64 = sb("ones64", [128, 64], F32)
        b_all = sb("b_all", [128, D], F32)
        gamma_all = sb("gamma_all", [128, D], F32)
        beta_all = sb("beta_all", [128, D], F32)
        wg_t = sb("wg_t", [128, HB, 128], F32)
        wu_t = sb("wu_t", [128, HB, 128], F32)
        wd_t = sb("wd_t", [128, HB, 128], F32)
        stage = probs[:, :, :, :].rearrange("p r h n -> p (r h n)")
        w_stage = [stage[:, k * HD:(k + 1) * HD] for k in range(3)]
        ffn_int = [stage[:, 3 * HD + k * HIDDEN:3 * HD + (k + 1) * HIDDEN].bitcast(I32) for k in range(3)]
        ffn_f = [stage[:, 3 * HD + (3 + k) * HIDDEN:3 * HD + (4 + k) * HIDDEN] for k in range(3)]
        x1_buf = [stage[:, s * GROUP:(s + 1) * GROUP] for s in range(2)]
        x1_t = [stage[:, (2 + s) * GROUP:(3 + s) * GROUP] for s in range(2)]
        sil = stage[:, 4 * GROUP:(4 + HB) * GROUP]
        h_buf = stage[:, (4 + HB) * GROUP:(4 + 2 * HB) * GROUP]
        t_buf, r1_buf, r2_buf, out_buf = ([m[:, s * GROUP:(s + 1) * GROUP] for s in range(2)]
                                          for m in (o_raw[0], o_norm, row_sum, row_inv))
        parts = [[sb(f"parts{k}{s}", [128, GT, 6], F32) for s in range(2)] for k in range(3)]
        mean_var = [[sb(f"mean_var{k}{s}", [128, GT, 2], F32) for s in range(2)] for k in range(3)]
        rstd = [[sb(f"rstd{k}{s}", [128, GT], F32) for s in range(2)] for k in range(3)]
        minus_half = sb("minus_half", [128, GT], F32)
        EPS = (1e-6, 1e-5, 1e-5)
        eps_tile = [sb(f"eps_tile{k}", [128, GT], F32) for k in range(3)]

        ps = ctx.enter_context(nc.psum_tensor("ps", [128, 4096], F32))
        score_ps = [ps[:, h * S:(h + 1) * S] for h in range(2)]
        o_ps = ps[:, 2048:3072]
        side = ps[:, 3072:4096]
        side_bank = [ps[:, 3072:3584], ps[:, 3584:4096]]
        gate_ps = ps[:, 0:HB * GROUP]
        up_ps = ps[:, HB * GROUP:2 * HB * GROUP]
        turn_ps, down_ps = side_bank

        x_loaded = [sem(f"x_loaded{b}") for b in range(B)]
        qkv_loaded = sem("qkv_loaded")
        ffn_loaded = sem("ffn_loaded")
        vec_loaded = sem("vec_loaded")
        wp_loaded = sem("wp_loaded")
        made = sem("made")
        consts = sem("consts")
        padded = sem("padded")
        x_turned = sem("x_turned")
        x_high = sem("x_high")
        x_low = sem("x_low")
        w_high = sem("w_high")
        w_low = sem("w_low")
        y_begun = sem("y_begun")
        ffn_cast = sem("ffn_cast")
        ffn_turned = sem("ffn_turned")
        ffn_kept = sem("ffn_kept")
        w_here = [sem(f"w_here{s}") for s in range(2)]
        wp_here = [sem(f"wp_here{s}") for s in range(2)]
        x_here = sem("x_here")
        m_here = [sem(f"m_here{s}") for s in range(2)]
        q_proj = sem("q_proj")
        k_proj = sem("k_proj")
        v_proj = sem("v_proj")
        q_high = sem("q_high")
        k_high = sem("k_high")
        q_low = sem("q_low")
        k_low = sem("k_low")
        q_twin = sem("q_twin")
        k_twin = sem("k_twin")
        v_kept = sem("v_kept")
        max_scores = sem("max_scores")
        row_max = sem("row_max")
        m_joined = sem("m_joined")
        m_turned = sem("m_turned")
        m_rows = sem("m_rows")
        scores = sem("scores")
        exped = sem("exped")
        weighed = sem("weighed")
        summed = sem("summed")
        o_kept = sem("o_kept")
        sum_spread = sem("sum_spread")
        sum_kept = sem("sum_kept")
        inverted = sem("inverted")
        o_normed = sem("o_normed")
        projected = sem("projected")
        y_added = sem("y_added")
        norm_parts = [sem(f"norm_parts{k}") for k in range(3)]
        parts_seen = sem("parts_seen")
        norm_stats = [sem(f"norm_stats{k}") for k in range(3)]
        eps_added = [sem(f"eps_added{k}") for k in range(3)]
        rstd_done = [sem(f"rstd_done{k}") for k in range(3)]
        t_ready = sem("t_ready")
        gamma_done = sem("gamma_done")
        r1_ready = sem("r1_ready")
        x1_ready = sem("x1_ready")
        x1_turned = sem("x1_turned")
        x1_t_kept = sem("x1_t_kept")
        gated = sem("gated")
        silu_done = sem("silu_done")
        h_ready = sem("h_ready")
        downed = sem("downed")
        r2_ready = sem("r2_ready")
        out_ready = sem("out_ready")
        stored = [sem(f"stored{s}") for s in range(2)]
        NSUM = 2 * (KT - 1)
        LAST = PAIRS - 1

        MAX_TILES = {2: (0, 0, 0, 1, 2), 3: (1, 1, 1, 2, 2), 4: (1, 1, 0, 0, 2), 5: (1, 1, 1, 2, 2),
                     6: (1, 1, 1, 2, 2), 7: (1, 1, 1, 1, 0)}
        O_AT = (4, 3)
        O_TILES = 12
        assert sum(map(sum, MAX_TILES.values())) == MAXJ

        block = ctx.enter_context(nc.Block())

        class Pair:

            def __init__(self, eng, i, off):
                self.eng, self.i, self.off, self.kept = eng, i, off, {}

            def times(self, n, more=0):
                if isinstance(self.i, int):
                    return (2 * self.i + self.off) * n + more
                if n not in self.kept:
                    self.kept[n] = self.eng.snap(self.i * (2 * n))
                return self.kept[n] + (self.off * n + more)

            def second(self, n, more=0):
                if isinstance(self.i, int):
                    return (2 * self.i + self.off) // 2 * n + more
                key = ("half", n)
                if key not in self.kept:
                    self.kept[key] = self.eng.snap(self.i * n)
                return self.kept[key] + (self.off // 2 * n + more)

            def batch(self, n, more=0):
                if isinstance(self.i, int):
                    return (2 * self.i + self.off) // PB * n + more
                return self.eng.snap((self.i + self.off // 2) // (PB // 2) * n + more)

            def step(self, by):
                other = Pair(self.eng, self.i, self.off + by)
                other.kept = self.kept
                return other

            def batch_cols(self):
                if isinstance(self.i, int):
                    b = (2 * self.i + self.off) // PB
                    return slice(b * S, (b + 1) * S)
                return bass.ds(self.eng.snap((self.i + self.off // 2) // (PB // 2) * S), S)

            def cols(self):
                if isinstance(self.i, int):
                    g = 2 * self.i + self.off
                    return slice(g * GROUP, (g + 1) * GROUP)
                return bass.ds(self.times(GROUP), GROUP)

            @property
            def early(self):
                return isinstance(self.i, int) and 2 * self.i + self.off < 2

            @property
            def parity(self):
                return self.off % 2

        def over_pairs(eng, pair):
            for k in range(3):
                pair(Pair(eng, k // 2, k % 2), k, False)
            with eng.Fori(1, (PAIRS - 2) // 2) as i:
                kept = {}
                for off in (1, 2):
                    this = Pair(eng, i, off)
                    this.kept = kept
                    pair(this, 2, False)
            pair(Pair(eng, LAST // 2, LAST % 2), 2, True)

        def over_groups(eng, first_norm, second_norm, third_norm):
            def step(i, off, ahead):
                kept = {}
                for work, by in ((first_norm, 2), (second_norm, 1), (third_norm, 0)):
                    if work and by <= ahead:
                        g = Pair(eng, i, off + by)
                        g.kept = kept
                        work(g)
            if first_norm:
                first_norm(Pair(eng, 0, 0))
                first_norm(Pair(eng, 0, 1))
            if second_norm:
                second_norm(Pair(eng, 0, 0))
            step(0, 0, 2)
            step(0, 1, 2)
            with eng.Fori(1, GROUPS // 2 - 1) as i:
                step(i, 0, 2)
                step(i, 1, 2)
            step(GROUPS // 2 - 1, 0, 1)
            step(GROUPS // 2 - 1, 1, 0)

        first_row = [64, 0]

        x_t = x.rearrange("b (t p) d -> b p t d", p=128)
        out_g = out.rearrange("b (c t p) d -> (b c) p t d", p=128, t=GT)

        @block.sync
        def _(sp):
            for b in range(B):
                sp.dma_start(x_tok[:, b * S:(b + 1) * S].rearrange("p (t d) -> p t d", d=D), x_t[b])\
                  .then_inc(x_loaded[b], 16)
            sp.wait_ge(w_high, 3)
            sp.wait_ge(w_low, 3)
            sp.dma_start(w_slot[0][:, :, :], w_split[:, 0, :, :]).then_inc(w_here[0], 16)
            sp.wait_ge(x_high, 1)
            sp.wait_ge(x_low, 1)
            sp.dma_start(x_slot[:, :, :], x_split[:, 0, :, :]).then_inc(x_here, 16)
            sp.wait_ge(wp_loaded, 16)
            sp.wait_ge(x_high, B)
            sp.wait_ge(x_low, B)

            def batch(b, first, last):
                n0 = b * PB if isinstance(b, int) else sp.snap(b * PB)
                for j in range(PB):
                    s = j % 2
                    if not (last and j == PB - 1):
                        if not (first and j == 0):
                            sp.wait_ge(v_proj, n0 + j)
                        sp.dma_start(w_slot[1 - s][:, :, :], w_split[:, (j + 1) % PB, :, :])\
                          .then_inc(w_here[1 - s], 16)
                    if j == PB - 1 and not last:
                        sp.wait_ge(v_proj, n0 + PB)
                        sp.dma_start(x_slot[:, :, :], x_split[:, bass.ds(b + 1, 1), :, :]
                                     .rearrange("p a l n -> p (a l) n")).then_inc(x_here, 16)
                    sp.wait_ge(m_rows, n0 + (j + 1))
                    if first and j < 2:
                        sp.wait_ge(padded, 8)
                    for h in range(2):
                        row = first_row[h]
                        sp.dma_start(q_lm[s][h][row:row + 1, :].rearrange("a (t n) -> a t n", n=128),
                                     max_rows[KT * h:KT * (h + 1), :])\
                          .then_inc(m_here[s], 16)
                    if not (first and j < 2):
                        sp.wait_ge(projected, n0 + (j - 1))
                    sp.dma_start(wp_slot[s][:, :], wp_all[:, j, :]).then_inc(wp_here[s], 16)

            batch(0, True, False)
            with sp.Fori(1, B - 1) as b:
                batch(b, False, False)
            batch(B - 1, False, True)

            with sp.Fori(0, GROUPS // 2) as i:
                for s in range(2):
                    sp.wait_ge(out_ready, i * 2 + (s + 1))
                    sp.dma_start(out_g[bass.ds(i * 2 + s, 1), :, :, :].rearrange("a p t d -> p (a t) d"),
                                 out_buf[s].rearrange("p (t d) -> p t d", d=D)).then_inc(stored[s], 16)
            for s in range(2):
                sp.wait_ge(stored[s], 16 * (GROUPS // 2))

        @block.gpsimd
        def _(pool):
            for k, m in enumerate((ident, neg_ident)):
                pool.memset(m[:, :], 0.0).then_inc(made, 1)
                pool.wait_ge(made, 2 * k + 1)
                pool.affine_select(out=m[:, :], in_=m[:, :], compare_op=ALU.not_equal, fill=-1.0 if k else 1.0,
                                   base=0, pattern=[[-1, 128]], channel_multiplier=1).then_inc(made, 1)
            pool.memset(ones64[:, :], 1.0).then_inc(consts, 1)
            pool.memset(minus_half[:, :], -0.5).then_inc(consts, 1)
            for k in range(3):
                pool.memset(eps_tile[k][:, :], EPS[k]).then_inc(consts, 1)
            pool.wait_ge(vec_loaded, 48)
            for b in range(B):
                cols = slice(b * S, (b + 1) * S)
                tiles = x_tok[:, cols].rearrange("p (t d) -> p t d", d=D)
                over = [128, KT, D]
                pool.wait_ge(x_loaded[b], 16)
                pool.tensor_tensor(y_tok[:, cols].rearrange("p (t d) -> p t d", d=D), tiles,
                                   b_all[:, :].unsqueeze(1).to_broadcast(over), ALU.add).then_inc(y_begun, 1)
                pool.wait_ge(x_turned, b + 1)
                pool.wait_ge(y_begun, 2 * b + 1)
                pool.tensor_tensor(tiles, tiles, beta_all[:, :].unsqueeze(1).to_broadcast(over), ALU.add)\
                    .then_inc(y_begun, 1)

            def norm_o(r, first):
                pool.wait_ge(inverted, r.times(KT, KT))
                pool.wait_ge(o_kept, r.times(1, 1))
                if not first:
                    pool.wait_ge(projected, r.times(1))
                pool.tensor_tensor(o_norm[:, :], o_raw[r.parity][:, :], row_inv[:, :], ALU.mult)\
                    .then_inc(o_normed, 1)

            def pair(p, behind, last):
                tot = prob_sum[p.parity]
                for kt in range(1, KT):
                    for h in range(2):
                        pool.wait_ge(exped, p.times(2 * KT, 2 * kt + h + 1))
                        if kt == 1 and behind == 2:
                            pool.wait_ge(sum_spread, p.times(1, -1))
                        if kt == 1:
                            a = probs[:, 0, h, :]
                        else:
                            pool.wait_ge(summed, p.times(NSUM, 2 * (kt - 2) + h + 1))
                            a = tot[:, h, :]
                        pool.tensor_tensor(tot[:, h, :], a, probs[:, kt % RING, h, :], ALU.add).then_inc(summed, 1)
                    if kt == 2 and behind == 2:
                        norm_o(p.step(-2), False)

            over_pairs(pool, pair)
            norm_o(Pair(pool, LAST // 2, LAST % 2 - 1), False)
            norm_o(Pair(pool, LAST // 2, LAST % 2), False)
            pool.wait_ge(consts, 5)

            def rstd_of(g, k, joined, done):
                s = g.parity
                pool.wait_ge(joined, g.times(1, 1))
                pool.tensor_tensor(rstd[k][s][:, :], mean_var[k][s][:, :, 1], eps_tile[k][:, :], ALU.add)\
                    .then_inc(eps_added[k], 1)
                pool.wait_ge(eps_added[k], g.times(1, 1))
                pool.tensor_tensor(rstd[k][s][:, :], rstd[k][s][:, :], minus_half[:, :], ALU.pow).then_inc(done, 1)

            def first_norm(g):
                rstd_of(g, 0, norm_stats[0], rstd_done[0])
                s = g.parity
                pool.wait_ge(t_ready, g.times(1, 1))
                tiles = t_buf[s].rearrange("p (t d) -> p t d", d=D)
                pool.tensor_tensor(tiles, tiles, gamma_all[:, :].unsqueeze(1).to_broadcast([128, GT, D]), ALU.mult)\
                    .then_inc(gamma_done, 1)
                pool.wait_ge(gamma_done, g.times(1, 1))
                pool.tensor_tensor(r1_buf[s], t_buf[s], x_tok[:, g.cols()], ALU.add).then_inc(r1_ready, 1)

            def second_norm(g):
                rstd_of(g, 1, norm_stats[1], rstd_done[1])

            def third_norm(g):
                rstd_of(g, 2, norm_stats[2], rstd_done[2])

            over_groups(pool, first_norm, second_norm, third_norm)

        @block.scalar
        def _(act):
            for k, w in enumerate((w_q, w_k, w_v)):
                act.dma_start(w_stage[k], w).then_inc(qkv_loaded, 16)
            for vec, all_ in ((b_proj, b_all), (ln_gamma, gamma_all), (ln_beta, beta_all)):
                act.dma_start(all_[:, :], vec.rearrange("(a n) -> a n", a=1).to_broadcast([128, D]))\
                   .then_inc(vec_loaded, 16)
            act.dma_start(wp_all[:, :, :], w_proj.rearrange("(j p) d -> p j d", p=128)).then_inc(wp_loaded, 16)
            for k, w in enumerate((w_gate, w_up)):
                act.dma_start(ffn_int[k].rearrange("p (j d) -> p j d", d=D), w.rearrange("(j p) d -> p j d", p=128))\
                   .then_inc(ffn_loaded, 16)
            act.dma_start(ffn_int[2], w_down).then_inc(ffn_loaded, 16)

            act.wait_ge(qkv_loaded, 48)
            for k in range(3):
                act.activation(w_split[:, :, 2 * k, :], w_stage[k].rearrange("p (j n) -> p j n", n=128),
                               ACT.Copy, scale=W_SCALE).then_inc(w_high, 1)
            for b in range(B):
                act.wait_ge(x_turned, b + 1)
                act.activation(x_split[:, b, 0, :], ps[:, b * S:(b + 1) * S], ACT.Copy).then_inc(x_high, 1)
            for k, w_t in enumerate((wg_t, wu_t, wd_t)):
                act.wait_ge(ffn_turned, k + 1)
                act.activation(w_t[:, :, :], ps[:, k * 512:k * 512 + HIDDEN].rearrange("p (j n) -> p j n", n=128),
                               ACT.Copy).then_inc(ffn_kept, 1)

            def keep_q(n):
                act.wait_ge(q_proj, n.times(1, 1))
                for h in range(2):
                    act.activation(q_hh[n.parity][h][ROWS[h], :], side[ROWS[h], :], ACT.Copy, scale=Q_SCALE)\
                       .then_inc(q_high, 1)

            def keep_k(n):
                act.wait_ge(k_proj, n.times(1, 1))
                for h in range(2):
                    act.activation(k_h1[n.parity][h][ROWS[h], :], side[ROWS[h], :], ACT.Copy, scale=1 / W_SCALE)\
                       .then_inc(k_high, 1)

            def keep_v(n):
                act.wait_ge(v_proj, n.times(1, 1))
                act.activation(v_slot[n.parity][:, :, :], side.rearrange("p (t n) -> p t n", n=128), ACT.Copy,
                               scale=1 / W_SCALE).then_inc(v_kept, 1)

            def keep_max_rows(n, first=False):
                act.wait_ge(m_turned, n.times(1, 1))
                if not first:
                    before = n.step(-1)
                    act.wait_ge(m_here[before.parity], before.second(32, 32))
                act.activation(max_rows[:, :], side[0:MAXJ // 2, 0:128], ACT.Copy).then_inc(m_rows, 1)

            def exp(p, kt, h, first):
                j = 2 * kt + h
                act.wait_ge(scores, p.times(2 * KT, j + 1))
                if kt >= RING:
                    act.wait_ge(weighed, p.times(KT, kt - RING + 1))
                    act.wait_ge(summed, p.times(NSUM, 2 * max(kt - RING - 1, 0) + h + 1))
                elif not first:
                    act.wait_ge(weighed, p.times(KT, kt - RING + 1))
                    act.wait_ge(summed, p.times(NSUM, 2 * (kt - RING) + h + 1))
                act.activation(probs[:, kt % RING, h, :], score_ps[h], ACT.Exp).then_inc(exped, 1)

            def keep_o(q, first):
                act.wait_ge(weighed, q.times(KT, KT))
                if not first:
                    act.wait_ge(o_normed, q.times(1, -1))
                act.activation(o_raw[q.parity][:, :], o_ps, ACT.Copy).then_inc(o_kept, 1)

            def keep_sum(q, first):
                act.wait_ge(sum_spread, q.times(1, 1))
                if not first:
                    act.wait_ge(inverted, q.times(KT))
                act.activation(row_sum[:, :], side, ACT.Copy).then_inc(sum_kept, 1)

            start = Pair(act, 0, 0)
            keep_q(start)
            keep_k(start)
            keep_v(start)
            keep_max_rows(start, True)

            def pair(p, behind, last):
                n, q = p.step(1), p.step(-1)
                first = behind == 0
                if not last:
                    keep_q(n)
                if behind:
                    keep_o(q, behind == 1)
                for kt in range(KT):
                    exp(p, kt, 0, first)
                    if kt == 2 and behind:
                        keep_sum(q, behind == 1)
                    exp(p, kt, 1, first)
                    if kt == 0 and not last:
                        keep_k(n)
                    if kt == 1 and not last:
                        keep_v(n)
                if not last:
                    keep_max_rows(n)

            over_pairs(act, pair)
            end = Pair(act, LAST // 2, LAST % 2)
            keep_o(end, False)
            keep_sum(end, False)

            def turn_kept(g):
                act.wait_ge(x1_turned, g.times(1, 1))
                act.activation(x1_t[g.parity], turn_ps, ACT.Copy).then_inc(x1_t_kept, 1)

            def silu(g):
                act.wait_ge(gated, g.times(1, 1))
                act.wait_ge(h_ready, g.times(1))
                act.activation(sil, gate_ps, ACT.Silu).then_inc(silu_done, 1)

            over_groups(act, None, turn_kept, silu)

        @block.tensor
        def _(pe):
            pe.wait_ge(made, 4)
            for b in range(B):
                pe.wait_ge(x_loaded[b], 16)
                for t in range(b * KT, (b + 1) * KT):
                    mm = pe.transpose(ps[:, t * 128:(t + 1) * 128], x_tok[:, t * D:(t + 1) * D], ident[:, :])
                mm.then_inc(x_turned, 1)
            pe.wait_ge(x_high, B)
            pe.wait_ge(x_low, B)
            pe.wait_ge(ffn_cast, 3)
            for k in range(3):
                for j in range(HB):
                    mm = pe.transpose(ps[:, k * 512 + j * 128:k * 512 + (j + 1) * 128],
                                      ffn_f[k][:, j * 128:(j + 1) * 128], ident[:, :])
                mm.then_inc(ffn_turned, 1)

            def project(n, k, done):
                w = w_slot[n.parity]
                for t, (wp, xp) in enumerate(((2 * k, 1), (2 * k + 1, 0), (2 * k, 0))):
                    for c in range(2):
                        mm = pe.matmul(side_bank[c], w[:, wp, :], x_slot[:, xp, c * 512:(c + 1) * 512],
                                       start=t == 0, stop=t == 2)
                mm.then_inc(done, 1)

            def project_q(n, first=False):
                pe.wait_ge(w_here[n.parity], n.second(16, 16))
                pe.wait_ge(x_here, n.batch(16, 16))
                if not first:
                    pe.wait_ge(m_rows, n.times(1))
                project(n, 0, q_proj)

            def project_k(n):
                pe.wait_ge(q_high, n.times(2, 2))
                pe.wait_ge(q_low, n.times(2, 2))
                project(n, 1, k_proj)

            def project_v(n):
                pe.wait_ge(k_high, n.times(2, 2))
                pe.wait_ge(k_low, n.times(2, 2))
                w = w_slot[n.parity]
                for t in range(KT):
                    for i, (wp, xp) in enumerate(((4, 1), (5, 0), (4, 0))):
                        mm = pe.matmul(side[:, t * 128:(t + 1) * 128], x_slot[:, xp, t * 128:(t + 1) * 128],
                                       w[:, wp, :], start=i == 0, stop=i == 2)
                mm.then_inc(v_proj, 1)

            def max_tiles(n, a, b):
                for c in range(a, b):
                    h, qt, half = c // (2 * KT), c // 2 % KT, c % 2
                    if c == 0:
                        pe.wait_ge(q_twin, n.times(2, 2))
                        pe.wait_ge(k_twin, n.times(2, 2))
                    if c >= 2:
                        pe.wait_ge(row_max, n.times(MAXJ, c - 1))
                    pe.matmul(side_bank[c % 2], q_hh[n.parity][h][:, qt * 128:(qt + 1) * 128],
                              k_hl[n.parity][h][:, half * 512:(half + 1) * 512], start=True, stop=True)\
                      .then_inc(max_scores, 1)

            def turn_max(n):
                pe.wait_ge(m_joined, n.times(1, 1))
                pe.matmul(side[0:MAXJ // 2, 0:128], max16[:, :], neg_ident[:, :], start=True, stop=True)\
                  .then_inc(m_turned, 1)

            def score_high(p, kt, h, first):
                j = 2 * kt + h
                if not (first and j < 2):
                    pe.wait_ge(exped, p.times(2 * KT, j - 1))
                s, keys = p.parity, slice(kt * 128, (kt + 1) * 128)
                for c in range(2):
                    pe.matmul(score_ps[h][:, c * 512:(c + 1) * 512], k_hl[s][h][:, keys],
                              q_hh[s][h][:, c * 512:(c + 1) * 512], start=True, stop=False)

            def score_low(p, kt, h):
                s, keys = p.parity, slice(kt * 128, (kt + 1) * 128)
                if kt == 0 and h == 0:
                    pe.wait_ge(m_here[s], p.second(32, 32))
                for c in range(2):
                    mm = pe.matmul(score_ps[h][:, c * 512:(c + 1) * 512], k_h1[s][h][:, keys],
                                   q_lm[s][h][:, c * 512:(c + 1) * 512], start=False, stop=True)
                mm.then_inc(scores, 1)

            def weigh(p, kt, first):
                pe.wait_ge(exped, p.times(2 * KT, 2 * kt + 2))
                if kt == 0:
                    pe.wait_ge(v_kept, p.times(1, 1))
                    if not first:
                        pe.wait_ge(o_kept, p.times(1))
                for c in range(2):
                    for h in range(2):
                        mm = pe.matmul(o_ps[ROWS[h], c * 512:(c + 1) * 512], v_slot[p.parity][:, kt, ROWS[h]],
                                       probs[:, kt % RING, h, c * 512:(c + 1) * 512],
                                       start=kt == 0, stop=kt == KT - 1)
                mm.then_inc(weighed, 1)

            def spread_sum(q):
                pe.wait_ge(summed, q.times(NSUM, NSUM))
                for c in range(2):
                    for h in range(2):
                        mm = pe.matmul(side[ROWS[h], c * 512:(c + 1) * 512], ones64[:, :],
                                       prob_sum[q.parity][:, h, c * 512:(c + 1) * 512], start=True, stop=True)
                mm.then_inc(sum_spread, 1)

            def project_o(q):
                pe.wait_ge(o_normed, q.times(1, 1))
                pe.wait_ge(wp_here[q.parity], q.second(16, 16))
                for t in range(KT):
                    mm = pe.matmul(side[:, t * D:(t + 1) * D], o_norm[:, t * 128:(t + 1) * 128],
                                   wp_slot[q.parity][:, :], start=True, stop=True)
                mm.then_inc(projected, 1)

            start = Pair(pe, 0, 0)
            pe.wait_ge(ffn_kept, 3)
            project_q(start, True)
            project_k(start)
            project_v(start)
            pe.wait_ge(v_kept, 1)
            max_tiles(start, 0, MAXJ)
            turn_max(start)
            pe.wait_ge(padded, 8)
            pe.wait_ge(consts, 1)
            pe.wait_ge(q_low, 2)

            def pair(p, behind, last):
                n, q, r = p.step(1), p.step(-1), p.step(-2)
                first = behind == 0
                c = 0
                for kt in range(KT):
                    score_high(p, kt, 0, first)
                    if kt == 0:
                        score_high(p, kt, 1, first)
                        if not last:
                            project_q(n)
                        if behind:
                            weigh(q, KT - 1, behind == 1)
                        score_low(p, kt, 0)
                        score_low(p, kt, 1)
                        if not last:
                            project_k(n)
                        continue
                    for point in range(5):
                        if point == 1:
                            score_low(p, kt, 0)
                        if point == 2:
                            score_high(p, kt, 1, first)
                        if point == 3:
                            score_low(p, kt, 1)
                        if point == 4:
                            weigh(p, kt - 1, first)
                            if kt == 1 and not last:
                                project_v(n)
                            if kt == KT - 1 and not last:
                                turn_max(n)
                        if kt == 2 and point == 1:
                            if last:
                                pe.wait_ge(m_rows, PAIRS)
                            else:
                                pe.wait_ge(v_kept, n.times(1, 1))
                            if behind:
                                spread_sum(q)
                        if (kt, point) == O_AT and behind == 2:
                            if last:
                                pe.wait_ge(sum_kept, q.times(1, 1))
                            else:
                                pe.wait_ge(row_max, n.times(MAXJ, c))
                            project_o(r)
                        more = MAX_TILES[kt][point] if kt >= 2 and not last else 0
                        if more:
                            if c == 0 and behind:
                                pe.wait_ge(sum_kept, q.times(1, 1))
                            if c == O_TILES and behind == 2:
                                pe.wait_ge(y_added, r.times(1, 1))
                            max_tiles(n, c, c + more)
                            c += more

            over_pairs(pe, pair)
            end = Pair(pe, LAST // 2, LAST % 2)
            before = end.step(-1)
            weigh(end, KT - 1, False)
            pe.wait_ge(y_added, LAST - 1)
            project_o(before)
            pe.wait_ge(y_added, LAST)
            spread_sum(end)
            pe.wait_ge(sum_kept, LAST + 1)
            project_o(end)

            def turn(g):
                pe.wait_ge(x1_ready, g.times(1, 1))
                pe.wait_ge(x1_t_kept, g.times(1))
                for t in range(GT):
                    mm = pe.transpose(turn_ps[:, t * 128:(t + 1) * 128], x1_buf[g.parity][:, t * D:(t + 1) * D],
                                      ident[:, :])
                mm.then_inc(x1_turned, 1)

            def gate_up(g):
                pe.wait_ge(x1_t_kept, g.times(1, 1))
                pe.wait_ge(h_ready, g.times(1))
                for w_t, dst in ((wg_t, gate_ps), (wu_t, up_ps)):
                    for j in range(HB):
                        mm = pe.matmul(dst[:, j * GROUP:(j + 1) * GROUP], w_t[:, j, :], x1_t[g.parity],
                                       start=True, stop=True)
                mm.then_inc(gated, 1)

            def down(g):
                pe.wait_ge(h_ready, g.times(1, 1))
                pe.wait_ge(r2_ready, g.times(1))
                for t in range(GT):
                    for j in range(HB):
                        mm = pe.matmul(down_ps[:, t * D:(t + 1) * D],
                                       h_buf[:, j * GROUP + t * 128:j * GROUP + (t + 1) * 128], wd_t[:, j, :],
                                       start=j == 0, stop=j == HB - 1)
                mm.then_inc(downed, 1)

            def second_norm(g):
                turn(g)

            def third_norm(g):
                gate_up(g)
                down(g)

            pe.wait_ge(y_added, PAIRS)
            over_groups(pe, None, second_norm, third_norm)

        @block.vector
        def _(dve):
            for s in range(2):
                for h in range(2):
                    other = ROWS[1 - h]
                    dve.memset(k_h1[s][h][other, :], 1.0).then_inc(padded, 1)
                    dve.memset(q_lm[s][h][other, :], 0.0).then_inc(padded, 1)
            dve.wait_ge(qkv_loaded, 48)
            for k in range(3):
                dve.wait_ge(w_high, k + 1)
                dve.scalar_tensor_tensor(out=w_split[:, :, 2 * k + 1, :],
                                         in0=w_stage[k].rearrange("p (j n) -> p j n", n=128), scalar=W_SCALE,
                                         in1=w_split[:, :, 2 * k, :], op0=ALU.mult, op1=ALU.subtract)\
                   .then_inc(w_low, 1)
            for b in range(B):
                dve.wait_ge(x_high, b + 1)
                dve.tensor_tensor(x_split[:, b, 1, :], ps[:, b * S:(b + 1) * S], x_split[:, b, 0, :], ALU.subtract)\
                   .then_inc(x_low, 1)
            dve.wait_ge(ffn_loaded, 48)
            for k in range(3):
                dve.tensor_scalar(ffn_f[k], ffn_int[k], 1.0 / 127.0, None, ALU.mult).then_inc(ffn_cast, 1)

            def part_q(n):
                s = n.parity
                dve.wait_ge(q_proj, n.times(1, 1))
                for h in range(2):
                    dve.wait_ge(q_high, n.times(2, h + 1))
                    dve.scalar_tensor_tensor(out=q_lm[s][h][ROWS[h], :], in0=side[ROWS[h], :], scalar=Q_SCALE,
                                             in1=q_hh[s][h][ROWS[h], :], op0=ALU.mult, op1=ALU.subtract)\
                       .then_inc(q_low, 1)
                for h in range(2):
                    dve.tensor_copy(q_hh[s][h][ROWS[1 - h], :], q_hh[s][h][ROWS[h], :]).then_inc(q_twin, 1)

            def part_k(n):
                s = n.parity
                dve.wait_ge(k_proj, n.times(1, 1))
                for h in range(2):
                    dve.wait_ge(k_high, n.times(2, h + 1))
                    dve.scalar_tensor_tensor(out=k_hl[s][h][ROWS[1 - h], :], in0=side[ROWS[h], :],
                                             scalar=1 / W_SCALE, in1=k_h1[s][h][ROWS[h], :], op0=ALU.mult,
                                             op1=ALU.subtract).then_inc(k_low, 1)
                for h in range(2):
                    dve.tensor_copy(k_hl[s][h][ROWS[h], :], k_h1[s][h][ROWS[h], :]).then_inc(k_twin, 1)

            def max_tile(n, c):
                dve.wait_ge(max_scores, n.times(MAXJ, c + 1))
                dve.tensor_reduce(tile_max[:, c // 2, c % 2:c % 2 + 1], side_bank[c % 2], AX_X, ALU.max)\
                   .then_inc(row_max, 1)

            def join_max(n, first=False):
                dve.wait_ge(row_max, n.times(MAXJ, MAXJ))
                if not first:
                    dve.wait_ge(m_turned, n.times(1))
                dve.tensor_tensor(max16[:, :], tile_max[:, :, 0], tile_max[:, :, 1], ALU.max).then_inc(m_joined, 1)

            def invert(q, part, first=False):
                dve.wait_ge(sum_kept, q.times(1, 1))
                if part == 0 and not first:
                    dve.wait_ge(o_normed, q.times(1))
                cols = slice(part * (S // KT), (part + 1) * (S // KT))
                dve.reciprocal(row_inv[:, cols], row_sum[:, cols]).then_inc(inverted, 1)

            def add_y(q):
                dve.wait_ge(projected, q.times(1, 1))
                y = y_tok[:, q.batch_cols()]
                dve.tensor_tensor(y, side, y, ALU.add).then_inc(y_added, 1)

            start = Pair(dve, 0, 0)
            part_q(start)
            part_k(start)
            for c in range(MAXJ):
                max_tile(start, c)
            join_max(start, True)
            dve.wait_ge(y_begun, 2 * B)

            def pair(p, behind, last):
                n, r = p.step(1), p.step(-2)
                for part in range(KT):
                    if behind == 2:
                        invert(r, part, False)
                    if part == 2 and not last:
                        part_q(n)
                    if part == 4 and not last:
                        part_k(n)
                for c in range(MAXJ):
                    if c == O_TILES and behind == 2:
                        add_y(r)
                    if not last:
                        max_tile(n, c)
                if not last:
                    join_max(n)

            over_pairs(dve, pair)
            end = Pair(dve, LAST // 2, LAST % 2)
            for q in (end.step(-1), end):
                for part in range(KT):
                    invert(q, part)
                add_y(q)
            dve.wait_ge(y_added, PAIRS)

            def stats_of(g, k, tiles):
                s = g.parity
                for t in range(GT):
                    dve.bn_stats(parts[k][s][:, t, :], tiles[:, t, :]).then_inc(norm_parts[k], 1)
                for t in range(GT):
                    if t == 0:
                        dve.wait_ge(norm_parts[k], g.times(GT, GT))
                        dve.sem_inc(parts_seen, 1)
                    last = dve.bn_aggr(mean_var[k][s][:, t, :], parts[k][s][:, t, :])
                last.then_inc(norm_stats[k], 1)

            def apply(g, k, dst, tiles, done):
                s = g.parity
                dve.wait_ge(rstd_done[k], g.times(1, 1))
                for t in range(GT):
                    last = dve.tensor_scalar(dst[:, t * D:(t + 1) * D], tiles[:, t, :], mean_var[k][s][:, t, 0:1],
                                             rstd[k][s][:, t:t + 1], ALU.subtract, ALU.mult)
                last.then_inc(done, 1)

            def split_tiles(a):
                return a.rearrange("p (t d) -> p t d", d=D)

            def first_norm(g):
                y = split_tiles(y_tok[:, g.cols()])
                stats_of(g, 0, y)
                apply(g, 0, t_buf[g.parity], y, t_ready)

            def second_norm(g):
                dve.wait_ge(r1_ready, g.times(1, 1))
                r1 = split_tiles(r1_buf[g.parity])
                stats_of(g, 1, r1)
                apply(g, 1, x1_buf[g.parity], r1, x1_ready)

            def third_norm(g):
                s = g.parity
                dve.wait_ge(silu_done, g.times(1, 1))
                dve.wait_ge(downed, g.times(1))
                dve.tensor_tensor(h_buf, up_ps, sil, ALU.mult).then_inc(h_ready, 1)
                dve.wait_ge(downed, g.times(1, 1))
                dve.tensor_tensor(r2_buf[s], down_ps, x1_buf[s], ALU.add).then_inc(r2_ready, 1)
                dve.wait_ge(r2_ready, g.times(1, 1))
                r2 = split_tiles(r2_buf[s])
                stats_of(g, 2, r2)
                if not g.early:
                    dve.wait_ge(stored[s], g.second(16))
                apply(g, 2, out_buf[s], r2, out_ready)

            over_groups(dve, first_norm, second_norm, third_norm)


_INS = ['L0_attn_x', 'L0_attn_w_q', 'L0_attn_w_k', 'L0_attn_w_v', 'L0_attn_w_proj', 'L0_attn_b_proj',
        'L0_attn_ln_gamma', 'L0_attn_ln_beta', 'L0_ffn_w_gate', 'L0_ffn_w_up', 'L0_ffn_w_down']
_OUTS = [((4, 1024, 128), 'float32')]


def kernel(**inputs):
    import numpy as _np
    import concourse.bacc as _bacc
    from concourse import mybir as _mybir
    from concourse.bass_utils import run_bass_kernel_spmd as _run

    nc = _bacc.Bacc("TRN2", target_bir_lowering=False, num_devices=1)
    arrays, args = {}, []
    for name in _INS:
        a = _np.ascontiguousarray(inputs[name])
        arrays[f"in_{name}_dram"] = a
        args.append(nc.dram_tensor(f"in_{name}_dram", a.shape, _mybir.dt.from_np(a.dtype), kind="ExternalInput").ap())
    for i, (shape, dtype) in enumerate(_OUTS):
        dt = _mybir.dt.from_np(_np.dtype(dtype))
        args.append(nc.dram_tensor(f"out_{i}_dram", shape, dt, kind="ExternalOutput").ap())
    attention_ffn_program(nc, *args)
    r = _run(nc, [arrays], core_ids=[0])
    return r.results[0]["out_0_dram"]
```

```python
from contextlib import ExitStack

import concourse.bass as bass
from concourse import mybir

F32 = mybir.dt.float32
F16 = mybir.dt.float16
I32 = mybir.dt.int32
ALU = mybir.AluOpType
ACT = mybir.ActivationFunctionType
AX_X = mybir.AxisListType.X

ROWS = (slice(0, 64), slice(64, 128))


def attention_ffn_program(nc, x, w_q, w_k, w_v, w_proj, b_proj, ln_gamma, ln_beta, w_gate, w_up, w_down, out):
    B, S, D = x.shape
    HD = w_q.shape[1]
    HIDDEN = w_gate.shape[0]
    DH = 64
    T = B * S
    TILES = T // 128
    KT = S // 128
    PB = HD // 128
    PAIRS = B * PB
    HB = HIDDEN // 128
    GROUP = 512
    GT = GROUP // 128
    GROUPS = T // GROUP
    RING = 4
    W_SCALE = 64.0
    Q_SCALE = DH ** -0.5 / W_SCALE
    MAXJ = 2 * KT * 2
    assert D == 128 and S == 1024 and DH * 2 == 128 and PB == 8

    with ExitStack() as ctx:
        def sb(name, shape, dt):
            return ctx.enter_context(nc.sbuf_tensor(name, shape, dt))

        def sem(name):
            return ctx.enter_context(nc.semaphore(name))

        x_tok = sb("x_tok", [128, T], F32)
        y_tok = sb("y_tok", [128, T], F32)
        x_split = sb("x_split", [128, B, 2, S], F16)
        w_split = sb("w_split", [128, PB, 6, 128], F16)
        wp_all = sb("wp_all", [128, PB, D], F32)
        x_slot = sb("x_slot", [128, 2, S], F16)
        w_slot = [sb(f"w_slot{s}", [128, 6, 128], F16) for s in range(2)]
        wp_slot = [sb(f"wp_slot{s}", [128, D], F32) for s in range(2)]
        q_hh = [[sb(f"q_hh{s}{h}", [128, S], F16) for h in range(2)] for s in range(2)]
        q_lm = [[sb(f"q_lm{s}{h}", [128, S], F16) for h in range(2)] for s in range(2)]
        k_hl = [[sb(f"k_hl{s}{h}", [128, S], F16) for h in range(2)] for s in range(2)]
        k_h1 = [[sb(f"k_h1{s}{h}", [128, S], F16) for h in range(2)] for s in range(2)]
        v_slot = [sb(f"v_slot{s}", [128, KT, 128], F32) for s in range(2)]
        probs = sb("probs", [128, RING, 2, S], F32)
        prob_sum = [sb(f"prob_sum{s}", [128, 2, S], F32) for s in range(2)]
        o_raw = [sb(f"o_raw{s}", [128, S], F32) for s in range(2)]
        o_norm = sb("o_norm", [128, S], F32)
        row_sum = sb("row_sum", [128, S], F32)
        row_inv = sb("row_inv", [128, S], F32)
        tile_max = sb("tile_max", [128, MAXJ // 2, 2], F32)
        max16 = sb("max16", [128, MAXJ // 2], F16)
        max_rows = sb("max_rows", [MAXJ // 2, 128], F16)
        ident = sb("ident", [128, 128], F32)
        neg_ident = sb("neg_ident", [128, 128], F16)
        ones64 = sb("ones64", [128, 64], F32)
        b_all = sb("b_all", [128, D], F32)
        gamma_all = sb("gamma_all", [128, D], F32)
        beta_all = sb("beta_all", [128, D], F32)
        wg_t = sb("wg_t", [128, HB, 128], F32)
        wu_t = sb("wu_t", [128, HB, 128], F32)
        wd_t = sb("wd_t", [128, HB, 128], F32)
        stage = probs[:, :, :, :].rearrange("p r h n -> p (r h n)")
        w_stage = [stage[:, k * HD:(k + 1) * HD] for k in range(3)]
        ffn_int = [stage[:, 3 * HD + k * HIDDEN:3 * HD + (k + 1) * HIDDEN].bitcast(I32) for k in range(3)]
        ffn_f = [stage[:, 3 * HD + (3 + k) * HIDDEN:3 * HD + (4 + k) * HIDDEN] for k in range(3)]
        x1_buf = [stage[:, s * GROUP:(s + 1) * GROUP] for s in range(2)]
        x1_t = [stage[:, (2 + s) * GROUP:(3 + s) * GROUP] for s in range(2)]
        sil = stage[:, 4 * GROUP:(4 + HB) * GROUP]
        h_buf = [stage[:, (4 + (1 + s) * HB) * GROUP:(4 + (2 + s) * HB) * GROUP] for s in range(2)]
        t_buf, r1_buf, r2_buf, out_buf = ([m[:, s * GROUP:(s + 1) * GROUP] for s in range(2)]
                                          for m in (o_raw[0], o_norm, row_sum, row_inv))
        parts = [[sb(f"parts{k}{s}", [128, GT, 6], F32) for s in range(2)] for k in range(3)]
        mean_var = [[sb(f"mean_var{k}{s}", [128, GT, 2], F32) for s in range(2)] for k in range(3)]
        rstd = [[sb(f"rstd{k}{s}", [128, GT], F32) for s in range(2)] for k in range(3)]
        shift = [[sb(f"shift{k}{s}", [128, GT], F32) for s in range(2)] for k in range(3)]
        zeros = sb("zeros", [128, GT], F32)
        minus_half = sb("minus_half", [128, GT], F32)
        EPS = (1e-6, 1e-5, 1e-5)
        eps_tile = [sb(f"eps_tile{k}", [128, GT], F32) for k in range(3)]

        ps = ctx.enter_context(nc.psum_tensor("ps", [128, 4096], F32))
        bank = [ps[:, k * 512:(k + 1) * 512] for k in range(8)]
        score_bank = bank[0:3]
        o_ps = ps[:, 3 * 512:5 * 512]
        side_bank = bank[5:8]
        side = ps[:, 5 * 512:7 * 512]
        gate_ps = bank[0:2 * HB:2]
        up_ps = bank[1:2 * HB:2]
        turn_ps, down_ps = bank[6:8]

        x_loaded = [sem(f"x_loaded{b}") for b in range(B)]
        qkv_loaded = sem("qkv_loaded")
        ffn_loaded = sem("ffn_loaded")
        vec_loaded = sem("vec_loaded")
        wp_loaded = sem("wp_loaded")
        made = sem("made")
        consts = sem("consts")
        padded = sem("padded")
        x_turned = sem("x_turned")
        x_high = sem("x_high")
        x_low = sem("x_low")
        w_high = sem("w_high")
        w_low = sem("w_low")
        y_begun = sem("y_begun")
        ffn_cast = sem("ffn_cast")
        ffn_turned = sem("ffn_turned")
        ffn_kept = sem("ffn_kept")
        w_here = [sem(f"w_here{s}") for s in range(2)]
        wp_here = [sem(f"wp_here{s}") for s in range(2)]
        x_here = sem("x_here")
        m_here = [sem(f"m_here{s}") for s in range(2)]
        q_proj = sem("q_proj")
        k_proj = sem("k_proj")
        v_proj = sem("v_proj")
        q_high = sem("q_high")
        k_high = sem("k_high")
        q_low = sem("q_low")
        k_low = sem("k_low")
        q_twin = sem("q_twin")
        k_twin = sem("k_twin")
        v_kept = sem("v_kept")
        max_scores = sem("max_scores")
        row_max = sem("row_max")
        m_joined = sem("m_joined")
        m_turned = sem("m_turned")
        m_rows = sem("m_rows")
        scores = sem("scores")
        exped = sem("exped")
        weighed = sem("weighed")
        summed = sem("summed")
        o_kept = sem("o_kept")
        sum_spread = sem("sum_spread")
        sum_kept = sem("sum_kept")
        inverted = sem("inverted")
        o_normed = sem("o_normed")
        projected = sem("projected")
        y_added = sem("y_added")
        norm_parts = [sem(f"norm_parts{k}") for k in range(3)]
        parts_seen = sem("parts_seen")
        norm_stats = [sem(f"norm_stats{k}") for k in range(3)]
        eps_added = [sem(f"eps_added{k}") for k in range(3)]
        mean_negated = [sem(f"mean_negated{k}") for k in range(3)]
        shift_done = [sem(f"shift_done{k}") for k in range(3)]
        rstd_done = [sem(f"rstd_done{k}") for k in range(3)]
        t_ready = sem("t_ready")
        gamma_done = sem("gamma_done")
        r1_ready = sem("r1_ready")
        x1_ready = sem("x1_ready")
        x1_turned = sem("x1_turned")
        x1_t_kept = sem("x1_t_kept")
        gated = sem("gated")
        silu_done = sem("silu_done")
        h_ready = sem("h_ready")
        downed = sem("downed")
        r2_ready = sem("r2_ready")
        out_ready = sem("out_ready")
        out_free = [sem(f"out_free{s}") for s in range(2)]
        NSUM = 2 * (KT - 1)
        LAST = PAIRS - 1

        MAX_TILES = {2: [2, 2, 2, 0, 1, 2],
                     3: [0, 1, 2, 0, 1, 2],
                     4: [2, None, None, 2, 2, 0],
                     5: [1, 2, 0, 1, 2, 0],
                     6: [1, 2, 0, 1, 2, 0],
                     7: [1, 2, 0, 1, None, None]}
        MAX_BANKS = [b for kt in sorted(MAX_TILES) for b in MAX_TILES[kt] if b is not None]
        SPREAD_AT = (2, 1)
        O_AT = (4, 2)
        O_TILES = sum(b is not None for kt in range(2, 5) for b in MAX_TILES[kt][:6 if kt < 4 else O_AT[1] + 1])
        TURN_AT = (7, 5)
        NSC = 4 * KT
        LAST_USE = [max(k for k in range(NSC) if k % 3 == b) for b in range(3)]
        assert len(MAX_BANKS) == MAXJ
        AFTER_SPREAD = next(c for c in range(MAXJ) if MAX_BANKS[c] < 2)
        AFTER_O = next(c for c in range(O_TILES, MAXJ) if MAX_BANKS[c] < 2)

        block = ctx.enter_context(nc.Block())

        class Pair:

            def __init__(self, eng, i, off):
                self.eng, self.i, self.off, self.kept = eng, i, off, {}

            def times(self, n, more=0):
                if isinstance(self.i, int):
                    return (2 * self.i + self.off) * n + more
                if n not in self.kept:
                    self.kept[n] = self.eng.snap(self.i * (2 * n))
                return self.kept[n] + (self.off * n + more)

            def second(self, n, more=0):
                if isinstance(self.i, int):
                    return (2 * self.i + self.off) // 2 * n + more
                key = ("half", n)
                if key not in self.kept:
                    self.kept[key] = self.eng.snap(self.i * n)
                return self.kept[key] + (self.off // 2 * n + more)

            def batch(self, n, more=0):
                if isinstance(self.i, int):
                    return (2 * self.i + self.off) // PB * n + more
                return self.eng.snap((self.i + self.off // 2) // (PB // 2) * n + more)

            def step(self, by):
                other = Pair(self.eng, self.i, self.off + by)
                other.kept = self.kept
                return other

            def batch_cols(self):
                if isinstance(self.i, int):
                    b = (2 * self.i + self.off) // PB
                    return slice(b * S, (b + 1) * S)
                return bass.ds(self.eng.snap((self.i + self.off // 2) // (PB // 2) * S), S)

            def cols(self):
                if isinstance(self.i, int):
                    g = 2 * self.i + self.off
                    return slice(g * GROUP, (g + 1) * GROUP)
                return bass.ds(self.times(GROUP), GROUP)

            @property
            def begin(self):
                return isinstance(self.i, int) and 2 * self.i + self.off < 1

            @property
            def early(self):
                return isinstance(self.i, int) and 2 * self.i + self.off < 2

            @property
            def parity(self):
                return self.off % 2

        def over_pairs(eng, pair):
            for k in range(3):
                pair(Pair(eng, k // 2, k % 2), k, False)
            with eng.Fori(1, (PAIRS - 2) // 2) as i:
                kept = {}
                for off in (1, 2):
                    this = Pair(eng, i, off)
                    this.kept = kept
                    pair(this, 2, False)
            pair(Pair(eng, LAST // 2, LAST % 2), 2, True)

        def over_groups(eng, step):
            def alone(number):
                step(Pair(eng, 0, number), lambda k: 0 <= number + k < GROUPS)

            for number in range(-2, 2):
                alone(number)
            with eng.Fori(1, GROUPS // 2 - 1) as i:
                kept = {}
                for off in range(2):
                    g = Pair(eng, i, off)
                    g.kept = kept
                    step(g, lambda k: True)
            for number in range(GROUPS - 2, GROUPS + 1):
                alone(number)

        def split_tiles(a):
            return a.rearrange("p (t d) -> p t d", d=D)

        first_row = [64, 0]

        x_t = x.rearrange("b (t p) d -> b p t d", p=128)
        out_g = out.rearrange("b (c t p) d -> (b c) p t d", p=128, t=GT)

        @block.sync
        def _(sp):
            for s in range(2):
                sp.sem_inc(out_free[s], 16)
            for b in range(B):
                sp.dma_start(x_tok[:, b * S:(b + 1) * S].rearrange("p (t d) -> p t d", d=D), x_t[b])\
                  .then_inc(x_loaded[b], 16)
            sp.wait_ge(w_high, 3)
            sp.wait_ge(w_low, 3)
            sp.dma_start(w_slot[0][:, :, :], w_split[:, 0, :, :]).then_inc(w_here[0], 16)
            sp.wait_ge(x_high, 1)
            sp.wait_ge(x_low, 1)
            sp.dma_start(x_slot[:, :, :], x_split[:, 0, :, :]).then_inc(x_here, 16)
            sp.wait_ge(wp_loaded, 16)
            sp.wait_ge(x_high, B)
            sp.wait_ge(x_low, B)

            def batch(b, first, last):
                n0 = b * PB if isinstance(b, int) else sp.snap(b * PB)
                for j in range(PB):
                    s = j % 2
                    if not (last and j == PB - 1):
                        if not (first and j == 0):
                            sp.wait_ge(v_proj, n0 + j)
                        sp.dma_start(w_slot[1 - s][:, :, :], w_split[:, (j + 1) % PB, :, :])\
                          .then_inc(w_here[1 - s], 16)
                    if j == PB - 1 and not last:
                        sp.wait_ge(v_proj, n0 + PB)
                        sp.dma_start(x_slot[:, :, :], x_split[:, bass.ds(b + 1, 1), :, :]
                                     .rearrange("p a l n -> p (a l) n")).then_inc(x_here, 16)
                    sp.wait_ge(m_rows, n0 + (j + 1))
                    if first and j < 2:
                        sp.wait_ge(padded, 8)
                    for h in range(2):
                        row = first_row[h]
                        sp.dma_start(q_lm[s][h][row:row + 1, :].rearrange("a (t n) -> a t n", n=128),
                                     max_rows[KT * h:KT * (h + 1), :])\
                          .then_inc(m_here[s], 16)
                    if not (first and j < 2):
                        sp.wait_ge(projected, n0 + (j - 1))
                    sp.dma_start(wp_slot[s][:, :], wp_all[:, j, :]).then_inc(wp_here[s], 16)

            batch(0, True, False)
            with sp.Fori(1, B - 1) as b:
                batch(b, False, False)
            batch(B - 1, False, True)

            with sp.Fori(0, GROUPS // 2) as i:
                for s in range(2):
                    sp.wait_ge(out_ready, i * 2 + (s + 1))
                    sp.dma_start(out_g[bass.ds(i * 2 + s, 1), :, :, :].rearrange("a p t d -> p (a t) d"),
                                 split_tiles(out_buf[s])).then_inc(out_free[s], 16)
            for s in range(2):
                sp.wait_ge(out_free[s], 16 + 16 * (GROUPS // 2))

        @block.gpsimd
        def _(pool):
            for k, m in enumerate((ident, neg_ident)):
                pool.memset(m[:, :], 0.0).then_inc(made, 1)
                pool.wait_ge(made, 2 * k + 1)
                pool.affine_select(out=m[:, :], in_=m[:, :], compare_op=ALU.not_equal, fill=-1.0 if k else 1.0,
                                   base=0, pattern=[[-1, 128]], channel_multiplier=1).then_inc(made, 1)
            pool.memset(ones64[:, :], 1.0).then_inc(consts, 1)
            pool.memset(minus_half[:, :], -0.5).then_inc(consts, 1)
            pool.memset(zeros[:, :], 0.0).then_inc(consts, 1)
            for k in range(3):
                pool.memset(eps_tile[k][:, :], EPS[k]).then_inc(consts, 1)
            pool.wait_ge(vec_loaded, 48)
            for b in range(B):
                cols = slice(b * S, (b + 1) * S)
                tiles = x_tok[:, cols].rearrange("p (t d) -> p t d", d=D)
                over = [128, KT, D]
                pool.wait_ge(x_loaded[b], 16)
                pool.tensor_tensor(y_tok[:, cols].rearrange("p (t d) -> p t d", d=D), tiles,
                                   b_all[:, :].unsqueeze(1).to_broadcast(over), ALU.add).then_inc(y_begun, 1)
                pool.wait_ge(x_turned, b + 1)
                pool.wait_ge(y_begun, 2 * b + 1)
                pool.tensor_tensor(tiles, tiles, beta_all[:, :].unsqueeze(1).to_broadcast(over), ALU.add)\
                    .then_inc(y_begun, 1)

            def norm_o(r, first):
                pool.wait_ge(inverted, r.times(KT, KT))
                pool.wait_ge(o_kept, r.times(1, 1))
                if not first:
                    pool.wait_ge(projected, r.times(1))
                pool.tensor_tensor(o_norm[:, :], o_raw[r.parity][:, :], row_inv[:, :], ALU.mult)\
                    .then_inc(o_normed, 1)

            def pair(p, behind, last):
                tot = prob_sum[p.parity]
                for kt in range(1, KT):
                    for h in range(2):
                        pool.wait_ge(exped, p.times(NSC, 4 * kt + 2 * h + 2))
                        if kt == 1 and behind == 2:
                            pool.wait_ge(sum_spread, p.times(1, -1))
                        if kt == 1:
                            a = probs[:, 0, h, :]
                        else:
                            pool.wait_ge(summed, p.times(NSUM, 2 * (kt - 2) + h + 1))
                            a = tot[:, h, :]
                        pool.tensor_tensor(tot[:, h, :], a, probs[:, kt % RING, h, :], ALU.add).then_inc(summed, 1)
                    if kt == 2 and behind == 2:
                        norm_o(p.step(-2), False)

            over_pairs(pool, pair)
            norm_o(Pair(pool, LAST // 2, LAST % 2 - 1), False)
            norm_o(Pair(pool, LAST // 2, LAST % 2), False)
            pool.wait_ge(consts, 6)

            def rstd_of(g, k, shifted):
                s = g.parity
                mean, var = mean_var[k][s][:, :, 0], mean_var[k][s][:, :, 1]
                pool.wait_ge(norm_stats[k], g.times(1, 1))
                pool.tensor_tensor(rstd[k][s][:, :], var, eps_tile[k][:, :], ALU.add).then_inc(eps_added[k], 1)
                if shifted:
                    pool.tensor_tensor(shift[k][s][:, :], zeros[:, :], mean, ALU.subtract)\
                        .then_inc(mean_negated[k], 1)
                pool.wait_ge(eps_added[k], g.times(1, 1))
                pool.tensor_tensor(rstd[k][s][:, :], rstd[k][s][:, :], minus_half[:, :], ALU.pow)\
                    .then_inc(rstd_done[k], 1)
                if shifted:
                    pool.wait_ge(mean_negated[k], g.times(1, 1))
                    pool.wait_ge(rstd_done[k], g.times(1, 1))
                    pool.tensor_tensor(shift[k][s][:, :], shift[k][s][:, :], rstd[k][s][:, :], ALU.mult)\
                        .then_inc(shift_done[k], 1)

            def add_x(g):
                s = g.parity
                pool.wait_ge(t_ready, g.times(1, 1))
                tiles = split_tiles(t_buf[s])
                pool.tensor_tensor(tiles, tiles, gamma_all[:, :].unsqueeze(1).to_broadcast([128, GT, D]), ALU.mult)\
                    .then_inc(gamma_done, 1)
                pool.wait_ge(gamma_done, g.times(1, 1))
                pool.tensor_tensor(r1_buf[s], t_buf[s], x_tok[:, g.cols()], ALU.add).then_inc(r1_ready, 1)

            def group(g, has):
                if has(1):
                    rstd_of(g.step(1), 1, False)
                if has(2):
                    rstd_of(g.step(2), 0, True)
                    add_x(g.step(2))
                if has(-1):
                    rstd_of(g.step(-1), 2, True)

            over_groups(pool, group)

        @block.scalar
        def _(act):
            for k, w in enumerate((w_q, w_k, w_v)):
                act.dma_start(w_stage[k], w).then_inc(qkv_loaded, 16)
            for vec, all_ in ((b_proj, b_all), (ln_gamma, gamma_all), (ln_beta, beta_all)):
                act.dma_start(all_[:, :], vec.rearrange("(a n) -> a n", a=1).to_broadcast([128, D]))\
                   .then_inc(vec_loaded, 16)
            act.dma_start(wp_all[:, :, :], w_proj.rearrange("(j p) d -> p j d", p=128)).then_inc(wp_loaded, 16)
            for k, w in enumerate((w_gate, w_up)):
                act.dma_start(ffn_int[k].rearrange("p (j d) -> p j d", d=D), w.rearrange("(j p) d -> p j d", p=128))\
                   .then_inc(ffn_loaded, 16)
            act.dma_start(ffn_int[2], w_down).then_inc(ffn_loaded, 16)

            act.wait_ge(qkv_loaded, 48)
            for k in range(3):
                act.activation(w_split[:, :, 2 * k, :], w_stage[k].rearrange("p (j n) -> p j n", n=128),
                               ACT.Copy, scale=W_SCALE).then_inc(w_high, 1)
            for b in range(B):
                act.wait_ge(x_turned, b + 1)
                act.activation(x_split[:, b, 0, :], ps[:, b * S:(b + 1) * S], ACT.Copy).then_inc(x_high, 1)
            for k, w_t in enumerate((wg_t, wu_t, wd_t)):
                act.wait_ge(ffn_turned, k + 1)
                act.activation(w_t[:, :, :], ps[:, k * 512:k * 512 + HIDDEN].rearrange("p (j n) -> p j n", n=128),
                               ACT.Copy).then_inc(ffn_kept, 1)

            def keep_q(n):
                act.wait_ge(q_proj, n.times(1, 1))
                for h in range(2):
                    act.activation(q_hh[n.parity][h][ROWS[h], :], side[ROWS[h], :], ACT.Copy, scale=Q_SCALE)\
                       .then_inc(q_high, 1)

            def keep_k(n, h):
                act.wait_ge(k_proj, n.times(1, 1))
                act.activation(k_h1[n.parity][h][ROWS[h], :], side[ROWS[h], :], ACT.Copy, scale=1 / W_SCALE)\
                   .then_inc(k_high, 1)

            def keep_v(n):
                act.wait_ge(v_proj, n.times(1, 1))
                act.activation(v_slot[n.parity][:, :, :], side.rearrange("p (t n) -> p t n", n=128), ACT.Copy,
                               scale=1 / W_SCALE).then_inc(v_kept, 1)

            def keep_max_rows(n, first=False):
                act.wait_ge(m_turned, n.times(1, 1))
                if not first:
                    before = n.step(-1)
                    act.wait_ge(m_here[before.parity], before.second(32, 32))
                act.activation(max_rows[:, :], side_bank[2][0:MAXJ // 2, 0:128], ACT.Copy).then_inc(m_rows, 1)

            def exp(p, kt, j, first):
                h, c = j // 2, j % 2
                act.wait_ge(scores, p.times(NSC, 4 * kt + j + 1))
                if c == 0 and kt >= RING:
                    act.wait_ge(weighed, p.times(KT, kt - RING + 1))
                    act.wait_ge(summed, p.times(NSUM, 2 * max(kt - RING - 1, 0) + h + 1))
                elif c == 0 and not first:
                    act.wait_ge(weighed, p.times(KT, kt - RING + 1))
                    act.wait_ge(summed, p.times(NSUM, 2 * (kt - RING) + h + 1))
                act.activation(probs[:, kt % RING, h, c * 512:(c + 1) * 512], score_bank[(4 * kt + j) % 3], ACT.Exp)\
                   .then_inc(exped, 1)

            def keep_o(q, first):
                act.wait_ge(weighed, q.times(KT, KT))
                if not first:
                    act.wait_ge(o_normed, q.times(1, -1))
                act.activation(o_raw[q.parity][:, :], o_ps, ACT.Copy).then_inc(o_kept, 1)

            def keep_sum(q, first):
                act.wait_ge(sum_spread, q.times(1, 1))
                if not first:
                    act.wait_ge(inverted, q.times(KT))
                act.activation(row_sum[:, :], side, ACT.Copy).then_inc(sum_kept, 1)

            start = Pair(act, 0, 0)
            keep_q(start)
            keep_k(start, 0)
            keep_k(start, 1)
            keep_v(start)
            keep_max_rows(start, True)

            def pair(p, behind, last):
                n, q = p.step(1), p.step(-1)
                first = behind == 0
                if not last:
                    keep_q(n)
                for kt in range(KT):
                    for j in range(4):
                        if kt == 1 and j < 2 and not last:
                            keep_k(n, j)
                        if kt == 2 and j == 2 and behind:
                            keep_sum(q, behind == 1)
                        exp(p, kt, j, first)
                    if kt == 0 and behind:
                        keep_o(q, behind == 1)
                    if kt == 1 and not last:
                        keep_v(n)
                if not last:
                    keep_max_rows(n)

            over_pairs(act, pair)
            end = Pair(act, LAST // 2, LAST % 2)
            keep_o(end, False)
            keep_sum(end, False)

            def apply(g, k, dst, src, done):
                s = g.parity
                act.wait_ge(shift_done[k], g.times(1, 1))
                for t in range(GT):
                    last = act.activation(dst[:, t, :], src[:, t, :], ACT.Identity, bias=shift[k][s][:, t:t + 1],
                                          scale=rstd[k][s][:, t:t + 1])
                last.then_inc(done, 1)

            def first_norm(g):
                if not g.early:
                    act.wait_ge(r1_ready, g.times(1, -1))
                apply(g, 0, split_tiles(t_buf[g.parity]), split_tiles(y_tok[:, g.cols()]), t_ready)

            def third_norm(g):
                s = g.parity
                act.wait_ge(out_free[s], g.second(16, 16))
                apply(g, 2, split_tiles(out_buf[s]), split_tiles(r2_buf[s]), out_ready)

            def turn_kept(g):
                act.wait_ge(x1_turned, g.times(1, 1))
                act.activation(x1_t[g.parity], turn_ps, ACT.Copy).then_inc(x1_t_kept, 1)

            def silu(g, j):
                act.wait_ge(gated, g.times(HB, j + 1))
                if not g.begin:
                    act.wait_ge(h_ready, g.times(HB, j + 1 - HB))
                act.activation(sil[:, j * GROUP:(j + 1) * GROUP], gate_ps[j], ACT.Silu).then_inc(silu_done, 1)

            def group(g, has):
                if has(0):
                    silu(g, 0)
                if has(2):
                    first_norm(g.step(2))
                if has(0):
                    silu(g, 1)
                if has(1):
                    turn_kept(g.step(1))
                if has(-1):
                    third_norm(g.step(-1))
                if has(0):
                    silu(g, 2)

            over_groups(act, group)

        @block.tensor
        def _(pe):
            pe.wait_ge(made, 4)
            for b in range(B):
                pe.wait_ge(x_loaded[b], 16)
                for t in range(b * KT, (b + 1) * KT):
                    mm = pe.transpose(ps[:, t * 128:(t + 1) * 128], x_tok[:, t * D:(t + 1) * D], ident[:, :])
                mm.then_inc(x_turned, 1)
            pe.wait_ge(x_high, B)
            pe.wait_ge(x_low, B)
            pe.wait_ge(ffn_cast, 3)
            for k in range(3):
                for j in range(HB):
                    mm = pe.transpose(ps[:, k * 512 + j * 128:k * 512 + (j + 1) * 128],
                                      ffn_f[k][:, j * 128:(j + 1) * 128], ident[:, :])
                mm.then_inc(ffn_turned, 1)

            def project(n, k, done):
                w = w_slot[n.parity]
                for t, (wp, xp) in enumerate(((2 * k, 1), (2 * k + 1, 0), (2 * k, 0))):
                    for c in range(2):
                        mm = pe.matmul(side_bank[c], w[:, wp, :], x_slot[:, xp, c * 512:(c + 1) * 512],
                                       start=t == 0, stop=t == 2)
                mm.then_inc(done, 1)

            def project_q(n, first=False):
                pe.wait_ge(w_here[n.parity], n.second(16, 16))
                pe.wait_ge(x_here, n.batch(16, 16))
                if not first:
                    pe.wait_ge(m_rows, n.times(1))
                project(n, 0, q_proj)

            def project_k(n):
                pe.wait_ge(q_high, n.times(2, 2))
                pe.wait_ge(q_low, n.times(2, 2))
                project(n, 1, k_proj)

            def project_v(n):
                pe.wait_ge(k_high, n.times(2, 2))
                pe.wait_ge(k_low, n.times(2, 2))
                w = w_slot[n.parity]
                for t in range(KT):
                    for i, (wp, xp) in enumerate(((4, 1), (5, 0), (4, 0))):
                        mm = pe.matmul(side[:, t * 128:(t + 1) * 128], x_slot[:, xp, t * 128:(t + 1) * 128],
                                       w[:, wp, :], start=i == 0, stop=i == 2)
                mm.then_inc(v_proj, 1)

            def max_tile(n, c):
                h, qt, half = c // (2 * KT), c // 2 % KT, c % 2
                if c == 0:
                    pe.wait_ge(q_twin, n.times(2, 2))
                    pe.wait_ge(k_twin, n.times(2, 2))
                if MAX_BANKS[c] in MAX_BANKS[:c]:
                    pe.wait_ge(row_max, n.times(MAXJ, c - MAX_BANKS[:c][::-1].index(MAX_BANKS[c])))
                pe.matmul(side_bank[MAX_BANKS[c]], q_hh[n.parity][h][:, qt * 128:(qt + 1) * 128],
                          k_hl[n.parity][h][:, half * 512:(half + 1) * 512], start=True, stop=True)\
                  .then_inc(max_scores, 1)

            def turn_max(n):
                pe.wait_ge(m_joined, n.times(1, 1))
                pe.matmul(side_bank[2][0:MAXJ // 2, 0:128], max16[:, :], neg_ident[:, :], start=True, stop=True)\
                  .then_inc(m_turned, 1)

            def score_high(p, kt, j, first):
                k, h, c = 4 * kt + j, j // 2, j % 2
                if k >= 3:
                    pe.wait_ge(exped, p.times(NSC, k - 2))
                elif not first:
                    pe.wait_ge(exped, p.times(NSC, LAST_USE[k] + 1 - NSC))
                s = p.parity
                pe.matmul(score_bank[k % 3], k_hl[s][h][:, kt * 128:(kt + 1) * 128],
                          q_hh[s][h][:, c * 512:(c + 1) * 512], start=True, stop=False)

            def score_low(p, kt, j):
                k, h, c = 4 * kt + j, j // 2, j % 2
                s = p.parity
                if k == 0:
                    pe.wait_ge(m_here[s], p.second(32, 32))
                pe.matmul(score_bank[k % 3], k_h1[s][h][:, kt * 128:(kt + 1) * 128],
                          q_lm[s][h][:, c * 512:(c + 1) * 512], start=False, stop=True).then_inc(scores, 1)

            def weigh(p, kt, c, first):
                pe.wait_ge(exped, p.times(NSC, 4 * kt + c + 3))
                if kt == 0 and c == 0:
                    pe.wait_ge(v_kept, p.times(1, 1))
                    if not first:
                        pe.wait_ge(o_kept, p.times(1))
                for h in range(2):
                    mm = pe.matmul(o_ps[ROWS[h], c * 512:(c + 1) * 512], v_slot[p.parity][:, kt, ROWS[h]],
                                   probs[:, kt % RING, h, c * 512:(c + 1) * 512],
                                   start=kt == 0, stop=kt == KT - 1)
                if c == 1:
                    mm.then_inc(weighed, 1)

            def spread_sum(q):
                pe.wait_ge(summed, q.times(NSUM, NSUM))
                for c in range(2):
                    for h in range(2):
                        mm = pe.matmul(side[ROWS[h], c * 512:(c + 1) * 512], ones64[:, :],
                                       prob_sum[q.parity][:, h, c * 512:(c + 1) * 512], start=True, stop=True)
                mm.then_inc(sum_spread, 1)

            def project_o(q):
                pe.wait_ge(o_normed, q.times(1, 1))
                pe.wait_ge(wp_here[q.parity], q.second(16, 16))
                for t in range(KT):
                    mm = pe.matmul(side[:, t * D:(t + 1) * D], o_norm[:, t * 128:(t + 1) * 128],
                                   wp_slot[q.parity][:, :], start=True, stop=True)
                mm.then_inc(projected, 1)

            start = Pair(pe, 0, 0)
            pe.wait_ge(ffn_kept, 3)
            project_q(start, True)
            project_k(start)
            project_v(start)
            pe.wait_ge(v_kept, 1)
            for c in range(MAXJ):
                max_tile(start, c)
            turn_max(start)
            pe.wait_ge(padded, 8)
            pe.wait_ge(consts, 1)
            pe.wait_ge(q_low, 2)

            def pair(p, behind, last):
                n, q, r = p.step(1), p.step(-1), p.step(-2)
                first = behind == 0
                c = 0
                for j in (2, 0, 1):
                    score_high(p, 0, j, first)
                if not last:
                    project_q(n)
                if behind:
                    weigh(q, KT - 1, 0, behind == 1)
                    weigh(q, KT - 1, 1, behind == 1)
                for j in range(3):
                    score_low(p, 0, j)
                score_high(p, 0, 3, first)
                score_low(p, 0, 3)
                if not last:
                    project_k(n)
                for kt in range(1, KT):
                    for point in range(6):
                        if point < 4:
                            score_high(p, kt, point, first)
                            score_low(p, kt, point)
                        else:
                            weigh(p, kt - 1, point - 4, first)
                        if kt >= 2 and not last and MAX_TILES[kt][point] is not None:
                            if behind and c == AFTER_SPREAD:
                                pe.wait_ge(sum_kept, q.times(1, 1))
                            if not behind and c == AFTER_SPREAD:
                                pe.wait_ge(v_kept, n.times(1, 1))
                            if behind == 2 and c == AFTER_O:
                                pe.wait_ge(y_added, r.times(1, 1))
                            max_tile(n, c)
                            c += 1
                        if (kt, point) == (1, 5) and not last:
                            project_v(n)
                        if (kt, point) == SPREAD_AT and behind:
                            if last:
                                pe.wait_ge(m_rows, PAIRS)
                            else:
                                pe.wait_ge(v_kept, n.times(1, 1))
                            spread_sum(q)
                        if (kt, point) == O_AT and behind == 2:
                            if last:
                                pe.wait_ge(sum_kept, q.times(1, 1))
                            else:
                                pe.wait_ge(row_max, n.times(MAXJ, c))
                            project_o(r)
                        if (kt, point) == TURN_AT and not last:
                            turn_max(n)

            over_pairs(pe, pair)
            end = Pair(pe, LAST // 2, LAST % 2)
            before = end.step(-1)
            weigh(end, KT - 1, 0, False)
            weigh(end, KT - 1, 1, False)
            pe.wait_ge(y_added, LAST - 1)
            project_o(before)
            pe.wait_ge(y_added, LAST)
            spread_sum(end)
            pe.wait_ge(sum_kept, LAST + 1)
            project_o(end)

            def turn(g):
                pe.wait_ge(x1_ready, g.times(1, 1))
                if not g.begin:
                    pe.wait_ge(x1_t_kept, g.times(1))
                for t in range(GT):
                    mm = pe.transpose(turn_ps[:, t * 128:(t + 1) * 128], x1_buf[g.parity][:, t * D:(t + 1) * D],
                                      ident[:, :])
                mm.then_inc(x1_turned, 1)

            def gate_up(g, j):
                if j == 0:
                    pe.wait_ge(x1_t_kept, g.times(1, 1))
                if not g.begin:
                    pe.wait_ge(h_ready, g.times(HB, j + 1 - HB))
                for w_t, dst in ((wg_t, gate_ps), (wu_t, up_ps)):
                    mm = pe.matmul(dst[j], w_t[:, j, :], x1_t[g.parity], start=True, stop=True)
                mm.then_inc(gated, 1)

            def down(g):
                pe.wait_ge(h_ready, g.times(HB, HB))
                if not g.begin:
                    pe.wait_ge(r2_ready, g.times(1))
                for t in range(GT):
                    for j in range(HB):
                        mm = pe.matmul(down_ps[:, t * D:(t + 1) * D],
                                       h_buf[g.parity][:, j * GROUP + t * 128:j * GROUP + (t + 1) * 128],
                                       wd_t[:, j, :], start=j == 0, stop=j == HB - 1)
                mm.then_inc(downed, 1)

            def group(g, has):
                if has(0):
                    gate_up(g, 0)
                if has(-1):
                    down(g.step(-1))
                if has(0):
                    gate_up(g, 1)
                if has(1):
                    turn(g.step(1))
                if has(0):
                    gate_up(g, 2)

            pe.wait_ge(y_added, PAIRS)
            over_groups(pe, group)

        @block.vector
        def _(dve):
            for s in range(2):
                for h in range(2):
                    other = ROWS[1 - h]
                    dve.memset(k_h1[s][h][other, :], 1.0).then_inc(padded, 1)
                    dve.memset(q_lm[s][h][other, :], 0.0).then_inc(padded, 1)
            dve.wait_ge(qkv_loaded, 48)
            for k in range(3):
                dve.wait_ge(w_high, k + 1)
                dve.scalar_tensor_tensor(out=w_split[:, :, 2 * k + 1, :],
                                         in0=w_stage[k].rearrange("p (j n) -> p j n", n=128), scalar=W_SCALE,
                                         in1=w_split[:, :, 2 * k, :], op0=ALU.mult, op1=ALU.subtract)\
                   .then_inc(w_low, 1)
            for b in range(B):
                dve.wait_ge(x_high, b + 1)
                dve.tensor_tensor(x_split[:, b, 1, :], ps[:, b * S:(b + 1) * S], x_split[:, b, 0, :], ALU.subtract)\
                   .then_inc(x_low, 1)
            dve.wait_ge(ffn_loaded, 48)
            for k in range(3):
                dve.tensor_scalar(ffn_f[k], ffn_int[k], 1.0 / 127.0, None, ALU.mult).then_inc(ffn_cast, 1)

            def part_q(n):
                s = n.parity
                dve.wait_ge(q_proj, n.times(1, 1))
                for h in range(2):
                    dve.wait_ge(q_high, n.times(2, h + 1))
                    dve.scalar_tensor_tensor(out=q_lm[s][h][ROWS[h], :], in0=side[ROWS[h], :], scalar=Q_SCALE,
                                             in1=q_hh[s][h][ROWS[h], :], op0=ALU.mult, op1=ALU.subtract)\
                       .then_inc(q_low, 1)
                for h in range(2):
                    dve.tensor_copy(q_hh[s][h][ROWS[1 - h], :], q_hh[s][h][ROWS[h], :]).then_inc(q_twin, 1)

            def part_k(n):
                s = n.parity
                dve.wait_ge(k_proj, n.times(1, 1))
                for h in range(2):
                    dve.wait_ge(k_high, n.times(2, h + 1))
                    dve.scalar_tensor_tensor(out=k_hl[s][h][ROWS[1 - h], :], in0=side[ROWS[h], :],
                                             scalar=1 / W_SCALE, in1=k_h1[s][h][ROWS[h], :], op0=ALU.mult,
                                             op1=ALU.subtract).then_inc(k_low, 1)
                for h in range(2):
                    dve.tensor_copy(k_hl[s][h][ROWS[h], :], k_h1[s][h][ROWS[h], :]).then_inc(k_twin, 1)

            def max_tile(n, c):
                dve.wait_ge(max_scores, n.times(MAXJ, c + 1))
                dve.tensor_reduce(tile_max[:, c // 2, c % 2:c % 2 + 1], side_bank[MAX_BANKS[c]], AX_X, ALU.max)\
                   .then_inc(row_max, 1)

            def join_max(n, first=False):
                dve.wait_ge(row_max, n.times(MAXJ, MAXJ))
                if not first:
                    dve.wait_ge(m_turned, n.times(1))
                dve.tensor_tensor(max16[:, :], tile_max[:, :, 0], tile_max[:, :, 1], ALU.max).then_inc(m_joined, 1)

            def invert(q, part, first=False):
                dve.wait_ge(sum_kept, q.times(1, 1))
                if part == 0 and not first:
                    dve.wait_ge(o_normed, q.times(1))
                cols = slice(part * (S // KT), (part + 1) * (S // KT))
                dve.reciprocal(row_inv[:, cols], row_sum[:, cols]).then_inc(inverted, 1)

            def add_y(q):
                dve.wait_ge(projected, q.times(1, 1))
                y = y_tok[:, q.batch_cols()]
                dve.tensor_tensor(y, side, y, ALU.add).then_inc(y_added, 1)

            start = Pair(dve, 0, 0)
            part_q(start)
            part_k(start)
            for c in range(MAXJ):
                max_tile(start, c)
            join_max(start, True)
            dve.wait_ge(y_begun, 2 * B)

            def pair(p, behind, last):
                n, r = p.step(1), p.step(-2)
                for part in range(KT - 1):
                    if behind == 2:
                        invert(r, part, False)
                    if part == 2 and not last:
                        part_q(n)
                    if part == 4 and not last:
                        part_k(n)
                for c in range(MAXJ):
                    if c == O_TILES and behind == 2:
                        add_y(r)
                    if not last:
                        max_tile(n, c)
                    if behind == 2 and c == 0:
                        invert(r, KT - 1, False)
                if not last:
                    join_max(n)

            over_pairs(dve, pair)
            end = Pair(dve, LAST // 2, LAST % 2)
            for q in (end.step(-1), end):
                for part in range(KT):
                    invert(q, part)
                add_y(q)
            dve.wait_ge(y_added, PAIRS)

            def stats_of(g, k, tiles):
                s = g.parity
                for t in range(GT):
                    dve.bn_stats(parts[k][s][:, t, :], tiles[:, t, :]).then_inc(norm_parts[k], 1)
                for t in range(GT):
                    if t == 0:
                        dve.wait_ge(norm_parts[k], g.times(GT, GT))
                        dve.sem_inc(parts_seen, 1)
                    last = dve.bn_aggr(mean_var[k][s][:, t, :], parts[k][s][:, t, :])
                last.then_inc(norm_stats[k], 1)

            def first_norm(g):
                stats_of(g, 0, split_tiles(y_tok[:, g.cols()]))

            def second_stats(g):
                dve.wait_ge(r1_ready, g.times(1, 1))
                stats_of(g, 1, split_tiles(r1_buf[g.parity]))

            def second_apply(g):
                s = g.parity
                dve.wait_ge(rstd_done[1], g.times(1, 1))
                if not g.early:
                    dve.wait_ge(x1_turned, g.times(1, -1))
                    dve.wait_ge(r2_ready, g.times(1, -1))
                for t in range(GT):
                    cols = slice(t * D, (t + 1) * D)
                    last = dve.tensor_scalar(x1_buf[s][:, cols], r1_buf[s][:, cols], mean_var[1][s][:, t, 0:1],
                                             rstd[1][s][:, t:t + 1], ALU.subtract, ALU.mult)
                last.then_inc(x1_ready, 1)

            def hidden(g, j):
                dve.wait_ge(silu_done, g.times(HB, j + 1))
                if not g.early:
                    dve.wait_ge(downed, g.times(1, -1))
                cols = slice(j * GROUP, (j + 1) * GROUP)
                dve.tensor_tensor(h_buf[g.parity][:, cols], up_ps[j], sil[:, cols], ALU.mult).then_inc(h_ready, 1)

            def add_x1(g):
                s = g.parity
                dve.wait_ge(downed, g.times(1, 1))
                if not g.early:
                    dve.wait_ge(out_ready, g.times(1, -1))
                dve.tensor_tensor(r2_buf[s], down_ps, x1_buf[s], ALU.add).then_inc(r2_ready, 1)

            def third_stats(g):
                dve.wait_ge(r2_ready, g.times(1, 1))
                stats_of(g, 2, split_tiles(r2_buf[g.parity]))

            def group(g, has):
                if has(1):
                    second_stats(g.step(1))
                if has(2):
                    first_norm(g.step(2))
                if has(0):
                    hidden(g, 0)
                if has(-1):
                    add_x1(g.step(-1))
                if has(1):
                    second_apply(g.step(1))
                if has(-1):
                    third_stats(g.step(-1))
                if has(0):
                    hidden(g, 1)
                    hidden(g, 2)

            over_groups(dve, group)


_INS = ['L0_attn_x', 'L0_attn_w_q', 'L0_attn_w_k', 'L0_attn_w_v', 'L0_attn_w_proj', 'L0_attn_b_proj',
        'L0_attn_ln_gamma', 'L0_attn_ln_beta', 'L0_ffn_w_gate', 'L0_ffn_w_up', 'L0_ffn_w_down']
_OUTS = [((4, 1024, 128), 'float32')]


def kernel(**inputs):
    import numpy as _np
    import concourse.bacc as _bacc
    from concourse import mybir as _mybir
    from concourse.bass_utils import run_bass_kernel_spmd as _run

    nc = _bacc.Bacc("TRN2", target_bir_lowering=False, num_devices=1)
    arrays, args = {}, []
    for name in _INS:
        a = _np.ascontiguousarray(inputs[name])
        arrays[f"in_{name}_dram"] = a
        args.append(nc.dram_tensor(f"in_{name}_dram", a.shape, _mybir.dt.from_np(a.dtype), kind="ExternalInput").ap())
    for i, (shape, dtype) in enumerate(_OUTS):
        dt = _mybir.dt.from_np(_np.dtype(dtype))
        args.append(nc.dram_tensor(f"out_{i}_dram", shape, dt, kind="ExternalOutput").ap())
    attention_ffn_program(nc, *args)
    r = _run(nc, [arrays], core_ids=[0])
    return r.results[0]["out_0_dram"]
```

```python
from contextlib import ExitStack

import concourse.bass as bass
from concourse import mybir

F32 = mybir.dt.float32
F16 = mybir.dt.float16
I32 = mybir.dt.int32
ALU = mybir.AluOpType
ACT = mybir.ActivationFunctionType
AX_X = mybir.AxisListType.X

ROWS = (slice(0, 64), slice(64, 128))


def attention_ffn_program(nc, x, w_q, w_k, w_v, w_proj, b_proj, ln_gamma, ln_beta, w_gate, w_up, w_down, out):
    B, S, D = x.shape
    HD = w_q.shape[1]
    HIDDEN = w_gate.shape[0]
    DH = 64
    T = B * S
    TILES = T // 128
    KT = S // 128
    PB = HD // 128
    PAIRS = B * PB
    HB = HIDDEN // 128
    GROUP = 512
    GT = GROUP // 128
    GROUPS = T // GROUP
    RING = 4
    W_SCALE = 64.0
    Q_SCALE = DH ** -0.5 / W_SCALE
    MAXJ = 2 * KT * 2
    assert D == 128 and S == 1024 and DH * 2 == 128 and PB == 8

    with ExitStack() as ctx:
        def sb(name, shape, dt):
            return ctx.enter_context(nc.sbuf_tensor(name, shape, dt))

        def sem(name):
            return ctx.enter_context(nc.semaphore(name))

        x_tok = sb("x_tok", [128, T], F32)
        y_tok = sb("y_tok", [128, T], F32)
        x_split = sb("x_split", [128, B, 2, S], F16)
        w_split = sb("w_split", [128, PB, 6, 128], F16)
        wp_all = sb("wp_all", [128, PB, D], F32)
        x_slot = sb("x_slot", [128, 2, S], F16)
        w_slot = [sb(f"w_slot{s}", [128, 6, 128], F16) for s in range(2)]
        wp_slot = [sb(f"wp_slot{s}", [128, D], F32) for s in range(2)]
        q_pair = [sb(f"q_pair{part}", [128, S], F16) for part in range(2)]
        k_high_pair = sb("k_high_pair", [128, S], F16)
        q_hh = [[sb(f"q_hh{s}{h}", [128, S], F16) for h in range(2)] for s in range(2)]
        q_lm = [[sb(f"q_lm{s}{h}", [128, S], F16) for h in range(2)] for s in range(2)]
        k_hl = [[sb(f"k_hl{s}{h}", [128, S], F16) for h in range(2)] for s in range(2)]
        k_h1 = [[sb(f"k_h1{s}{h}", [128, S], F16) for h in range(2)] for s in range(2)]
        v_slot = [sb(f"v_slot{s}", [128, KT, 128], F32) for s in range(2)]
        probs = sb("probs", [128, RING, 2, S], F32)
        prob_sum = [sb(f"prob_sum{s}", [128, 2, S], F32) for s in range(2)]
        sum_split = sb("sum_split", [128, 2, 2, S], F16)
        o_raw = [sb(f"o_raw{s}", [128, S], F32) for s in range(2)]
        o_norm = sb("o_norm", [128, S], F32)
        k_pair = [k_high_pair[:, :], o_norm[:, 0:S // 2].bitcast(F16)]
        row_sum = [sb(f"row_sum{s}", [128, S], F32) for s in range(2)]
        row_inv = sb("row_inv", [128, S], F32)
        tile_max = sb("tile_max", [128, MAXJ // 2, 2], F32)
        max16 = sb("max16", [128, MAXJ // 2], F16)
        max_rows = sb("max_rows", [MAXJ // 2, 128], F16)
        ident = sb("ident", [128, 128], F32)
        neg_ident = sb("neg_ident", [128, 128], F16)
        ones64 = sb("ones64", [128, 64], F16)
        b_all = sb("b_all", [128, D], F32)
        gamma_all = sb("gamma_all", [128, D], F32)
        beta_all = sb("beta_all", [128, D], F32)
        wg_t = sb("wg_t", [128, HB, 128], F32)
        wu_t = sb("wu_t", [128, HB, 128], F32)
        wd_t = sb("wd_t", [128, HB, 128], F32)
        stage = probs[:, :, :, :].rearrange("p r h n -> p (r h n)")
        w_stage = [stage[:, k * HD:(k + 1) * HD] for k in range(3)]
        ffn_int = [stage[:, 3 * HD + k * HIDDEN:3 * HD + (k + 1) * HIDDEN].bitcast(I32) for k in range(3)]
        ffn_f = [stage[:, 3 * HD + (3 + k) * HIDDEN:3 * HD + (4 + k) * HIDDEN] for k in range(3)]
        sil = stage[:, 0:HB * GROUP]
        h_buf = [stage[:, (1 + s) * HB * GROUP:(2 + s) * HB * GROUP] for s in range(2)]
        x1_buf = [q_hh[0][s][:, :].bitcast(F32) for s in range(2)]
        x1_t = [q_lm[0][s][:, :].bitcast(F32) for s in range(2)]
        spare = x_split[:, :, :, :].rearrange("p b l n -> p (b l n)").bitcast(F32)
        t_buf, r1_buf, r2_buf, out_buf = ([spare[:, (2 * k + s) * GROUP:(2 * k + s + 1) * GROUP] for s in range(2)]
                                          for k in range(4))
        parts = [[sb(f"parts{k}{s}", [128, GT, 6], F32) for s in range(2)] for k in range(3)]
        mean_var = [[sb(f"mean_var{k}{s}", [128, GT, 2], F32) for s in range(2)] for k in range(3)]
        rstd = [[sb(f"rstd{k}{s}", [128, GT], F32) for s in range(2)] for k in range(3)]
        shift = [[sb(f"shift{k}{s}", [128, GT], F32) for s in range(2)] for k in range(3)]
        zeros = sb("zeros", [128, GT], F32)
        minus_half = sb("minus_half", [128, GT], F32)
        EPS = (1e-6, 1e-5, 1e-5)
        eps_tile = [sb(f"eps_tile{k}", [128, GT], F32) for k in range(3)]

        ps = ctx.enter_context(nc.psum_tensor("ps", [128, 4096], F32))
        bank = [ps[:, k * 512:(k + 1) * 512] for k in range(8)]
        score_bank = bank[0:3]
        o_ps = ps[:, 3 * 512:5 * 512]
        side_bank = bank[5:8]
        side = ps[:, 5 * 512:7 * 512]
        x_ps = [ps[:, b % 2 * S:(b % 2 + 1) * S] for b in range(B)]
        ffn_ps = [bank[k][:, 0:HIDDEN] for k in (4, 0, 2)]
        gate_ps = bank[0:2 * HB:2]
        up_ps = bank[1:2 * HB:2]
        down_ps, turn_ps = bank[6:8]

        x_loaded = [sem(f"x_loaded{b}") for b in range(B)]
        qkv_loaded = [sem(f"qkv_loaded{k}") for k in range(3)]
        ffn_loaded = sem("ffn_loaded")
        vec_loaded = sem("vec_loaded")
        wp_loaded = sem("wp_loaded")
        made = sem("made")
        consts = sem("consts")
        padded = sem("padded")
        x_turned = sem("x_turned")
        x_high = sem("x_high")
        x_low = sem("x_low")
        w_high = sem("w_high")
        w_low = sem("w_low")
        y_begun = sem("y_begun")
        ffn_cast = sem("ffn_cast")
        ffn_turned = sem("ffn_turned")
        ffn_kept = sem("ffn_kept")
        w_here = [sem(f"w_here{s}") for s in range(2)]
        wp_here = [sem(f"wp_here{s}") for s in range(2)]
        x_here = sem("x_here")
        m_here = [sem(f"m_here{s}") for s in range(2)]
        q_proj = sem("q_proj")
        k_proj = sem("k_proj")
        v_proj = sem("v_proj")
        q_high = sem("q_high")
        k_high = sem("k_high")
        q_low = sem("q_low")
        k_low = sem("k_low")
        q_twin = sem("q_twin")
        k_twin = sem("k_twin")
        halves_here = [sem(f"halves_here{s}") for s in range(2)]
        v_kept = sem("v_kept")
        max_scores = sem("max_scores")
        row_max = sem("row_max")
        m_joined = sem("m_joined")
        m_turned = sem("m_turned")
        m_rows = sem("m_rows")
        scores = sem("scores")
        exped = sem("exped")
        weighed = sem("weighed")
        summed = sem("summed")
        o_kept = sem("o_kept")
        summed_late = sem("summed_late")
        sum_high = sem("sum_high")
        sum_low = sem("sum_low")
        sum_spread = sem("sum_spread")
        sum_kept = sem("sum_kept")
        inverted = sem("inverted")
        o_normed = sem("o_normed")
        projected = sem("projected")
        y_added = sem("y_added")
        end_normed = sem("end_normed")
        end_projected = sem("end_projected")
        end_added = sem("end_added")
        norm_parts = [sem(f"norm_parts{k}") for k in range(3)]
        parts_seen = sem("parts_seen")
        norm_stats = [sem(f"norm_stats{k}") for k in range(3)]
        eps_added = [sem(f"eps_added{k}") for k in range(3)]
        mean_negated = [sem(f"mean_negated{k}") for k in range(3)]
        shift_done = [sem(f"shift_done{k}") for k in range(3)]
        rstd_done = [sem(f"rstd_done{k}") for k in range(3)]
        t_ready = sem("t_ready")
        gamma_done = sem("gamma_done")
        r1_ready = sem("r1_ready")
        x1_ready = sem("x1_ready")
        x1_turned = sem("x1_turned")
        x1_t_kept = sem("x1_t_kept")
        gated = sem("gated")
        silu_done = sem("silu_done")
        h_ready = sem("h_ready")
        downed = sem("downed")
        r2_ready = sem("r2_ready")
        out_ready = sem("out_ready")
        out_free = [sem(f"out_free{s}") for s in range(2)]
        NSUM = 2 * (KT - 1)
        LAST = PAIRS - 1

        POINTS = (0, 1, "values 0", 2, 3, "values 1")
        MAX_TILES = {(2, 0): [2], (2, 2): [2], (2, 3): [2], (2, 5): [2],
                     (3, 0): [0], (3, 1): [1], (3, 2): [2, 0], (3, 3): [1], (3, 4): [2], (3, 5): [0],
                     (4, 0): [1], (4, 1): [2], (4, 3): [2], (4, 5): [2],
                     (5, 1): [0], (5, 2): [1, 2], (5, 3): [0], (5, 4): [1], (5, 5): [2, 0],
                     (6, 0): [1], (6, 1): [2], (6, 2): [0], (6, 3): [1], (6, 4): [2], (6, 5): [0, 1],
                     (7, 0): [2], (7, 1): [0], (7, 2): [1]}
        MAX_BANKS = [b for at in sorted(MAX_TILES) for b in MAX_TILES[at]]
        START_BANKS = [c % 3 for c in range(MAXJ)]
        assert len(MAX_BANKS) == MAXJ
        V_AT = (1, 5)
        SPREAD_AT = (2, 2)
        O_AT = (4, 3)
        O_TILES = sum(len(MAX_TILES[at]) for at in MAX_TILES if at <= O_AT)
        TURN_AT = (7, 5)
        LAST_O_AT = (7, 4)
        AFTER_SPREAD = next(c for c in range(MAXJ) if MAX_BANKS[c] < 2)
        BEFORE_O = max(c for c in range(O_TILES) if MAX_BANKS[c] < 2)
        AFTER_O = next(c for c in range(O_TILES, MAXJ) if MAX_BANKS[c] < 2)
        NSC = 4 * KT
        LAST_USE = [max(k for k in range(NSC) if k % 3 == b) for b in range(3)]

        block = ctx.enter_context(nc.Block())

        class Pair:

            def __init__(self, eng, i, off):
                self.eng, self.i, self.off, self.kept = eng, i, off, {}

            def times(self, n, more=0):
                if isinstance(self.i, int):
                    return (2 * self.i + self.off) * n + more
                if n not in self.kept:
                    self.kept[n] = self.eng.snap(self.i * (2 * n))
                return self.kept[n] + (self.off * n + more)

            def second(self, n, more=0):
                if isinstance(self.i, int):
                    return (2 * self.i + self.off) // 2 * n + more
                key = ("half", n)
                if key not in self.kept:
                    self.kept[key] = self.eng.snap(self.i * n)
                return self.kept[key] + (self.off // 2 * n + more)

            def batch(self, n, more=0):
                if isinstance(self.i, int):
                    return (2 * self.i + self.off) // PB * n + more
                return self.eng.snap((self.i + self.off // 2) // (PB // 2) * n + more)

            def step(self, by):
                other = Pair(self.eng, self.i, self.off + by)
                other.kept = self.kept
                return other

            def batch_cols(self):
                if isinstance(self.i, int):
                    b = (2 * self.i + self.off) // PB
                    return slice(b * S, (b + 1) * S)
                return bass.ds(self.eng.snap((self.i + self.off // 2) // (PB // 2) * S), S)

            def cols(self):
                if isinstance(self.i, int):
                    g = 2 * self.i + self.off
                    return slice(g * GROUP, (g + 1) * GROUP)
                return bass.ds(self.times(GROUP), GROUP)

            @property
            def number(self):
                return 2 * self.i + self.off if isinstance(self.i, int) else None

            @property
            def begin(self):
                return isinstance(self.i, int) and 2 * self.i + self.off < 1

            @property
            def early(self):
                return isinstance(self.i, int) and 2 * self.i + self.off < 2

            @property
            def parity(self):
                return self.off % 2

        def over_pairs(eng, pair, last_pair):
            for k in range(3):
                pair(Pair(eng, k // 2, k % 2), k, False)
            with eng.Fori(1, (PAIRS - 2) // 2) as i:
                kept = {}
                for off in (1, 2):
                    this = Pair(eng, i, off)
                    this.kept = kept
                    pair(this, 2, False)
            last_pair(Pair(eng, LAST // 2, LAST % 2))

        def over_groups(eng, step):
            def alone(number):
                step(Pair(eng, 0, number), lambda k: 0 <= number + k < GROUPS)

            alone(0)
            alone(1)
            with eng.Fori(1, GROUPS // 2 - 1) as i:
                kept = {}
                for off in range(2):
                    g = Pair(eng, i, off)
                    g.kept = kept
                    step(g, lambda k: True)
            for number in range(GROUPS - 2, GROUPS + 1):
                alone(number)

        def split_tiles(a):
            return a.rearrange("p (t d) -> p t d", d=D)

        first_row = [64, 0]

        x_t = x.rearrange("b (t p) d -> b p t d", p=128)
        out_g = out.rearrange("b (c t p) d -> (b c) p t d", p=128, t=GT)

        @block.sync
        def _(sp):
            for s in range(2):
                sp.sem_inc(out_free[s], 16)
            for b in range(B):
                sp.dma_start(x_tok[:, b * S:(b + 1) * S].rearrange("p (t d) -> p t d", d=D), x_t[b])\
                  .then_inc(x_loaded[b], 16)
            sp.wait_ge(w_high, 3)
            sp.wait_ge(w_low, 3)
            sp.sem_inc(w_here[0], 16)
            sp.wait_ge(x_high, 1)
            sp.wait_ge(x_low, 1)
            sp.dma_start(x_slot[:, :, :], x_split[:, 0, :, :]).then_inc(x_here, 16)
            sp.wait_ge(wp_loaded, 16)
            sp.wait_ge(x_high, B)
            sp.wait_ge(x_low, B)

            def batch(b, first, last):
                n0 = b * PB if isinstance(b, int) else sp.snap(b * PB)
                for j in range(PB):
                    s = j % 2
                    if not (last and j == PB - 1):
                        if not (first and j == 0):
                            sp.wait_ge(v_proj, n0 + j)
                        sp.dma_start(w_slot[1 - s][:, :, :], w_split[:, (j + 1) % PB, :, :])\
                          .then_inc(w_here[1 - s], 16)
                    for pair_of, part, done, dst in ((q_pair, 1, q_low, q_lm), (k_pair, 0, k_high, k_h1)):
                        sp.wait_ge(done, n0 + (j + 1))
                        for h in range(2):
                            sp.dma_start(dst[s][h][ROWS[h], :], pair_of[part][ROWS[h], :])\
                              .then_inc(halves_here[s], 16)
                    if j == PB - 1 and not last:
                        sp.wait_ge(v_proj, n0 + PB)
                        sp.dma_start(x_slot[:, :, :], x_split[:, bass.ds(b + 1, 1), :, :]
                                     .rearrange("p a l n -> p (a l) n")).then_inc(x_here, 16)
                    sp.wait_ge(m_rows, n0 + (j + 1))
                    if first and j < 2:
                        sp.wait_ge(padded, 8)
                    for h in range(2):
                        row = first_row[h]
                        sp.dma_start(q_lm[s][h][row:row + 1, :].rearrange("a (t n) -> a t n", n=128),
                                     max_rows[KT * h:KT * (h + 1), :])\
                          .then_inc(m_here[s], 16)
                    if not (first and j < 2):
                        sp.wait_ge(projected, n0 + (j - 1))
                    sp.dma_start(wp_slot[s][:, :], wp_all[:, j, :]).then_inc(wp_here[s], 16)

            batch(0, True, False)
            with sp.Fori(1, B - 1) as b:
                batch(b, False, False)
            batch(B - 1, False, True)

            with sp.Fori(0, GROUPS // 2) as i:
                for s in range(2):
                    sp.wait_ge(out_ready, i * 2 + (s + 1))
                    sp.dma_start(out_g[bass.ds(i * 2 + s, 1), :, :, :].rearrange("a p t d -> p (a t) d"),
                                 split_tiles(out_buf[s])).then_inc(out_free[s], 16)
            for s in range(2):
                sp.wait_ge(out_free[s], 16 + 16 * (GROUPS // 2))

        @block.gpsimd
        def _(pool):
            for k, m in enumerate((ident, neg_ident)):
                pool.memset(m[:, :], 0.0).then_inc(made, 1)
                pool.wait_ge(made, 2 * k + 1)
                pool.affine_select(out=m[:, :], in_=m[:, :], compare_op=ALU.not_equal, fill=-1.0 if k else 1.0,
                                   base=0, pattern=[[-1, 128]], channel_multiplier=1).then_inc(made, 1)
            pool.memset(ones64[:, :], 1.0).then_inc(consts, 1)
            pool.memset(minus_half[:, :], -0.5).then_inc(consts, 1)
            pool.memset(zeros[:, :], 0.0).then_inc(consts, 1)
            for k in range(3):
                pool.memset(eps_tile[k][:, :], EPS[k]).then_inc(consts, 1)
            pool.wait_ge(vec_loaded, 48)
            for b in range(B):
                cols = slice(b * S, (b + 1) * S)
                tiles = x_tok[:, cols].rearrange("p (t d) -> p t d", d=D)
                over = [128, KT, D]
                pool.wait_ge(x_loaded[b], 16)
                pool.tensor_tensor(y_tok[:, cols].rearrange("p (t d) -> p t d", d=D), tiles,
                                   b_all[:, :].unsqueeze(1).to_broadcast(over), ALU.add).then_inc(y_begun, 1)
                pool.wait_ge(x_turned, b + 1)
                pool.wait_ge(y_begun, 2 * b + 1)
                pool.tensor_tensor(tiles, tiles, beta_all[:, :].unsqueeze(1).to_broadcast(over), ALU.add)\
                    .then_inc(y_begun, 1)

            def norm_o(r, first):
                pool.wait_ge(inverted, r.times(KT, KT))
                pool.wait_ge(o_kept, r.times(1, 1))
                if not first:
                    pool.wait_ge(projected, r.times(1))
                pool.tensor_tensor(o_norm[:, :], o_raw[r.parity][:, :], row_inv[:, :], ALU.mult)\
                    .then_inc(o_normed, 1)

            def pair(p, behind, last):
                g0, g1 = Pair(pool, 0, 0), Pair(pool, 0, 1)
                tot = prob_sum[p.parity]
                for kt in range(1, KT):
                    for h in range(1 if last else 2):
                        pool.wait_ge(exped, p.times(NSC, 4 * kt + 2 * h + 2))
                        if kt == 1 and behind == 2:
                            pool.wait_ge(sum_spread, p.times(1, -1))
                        if kt == 1:
                            a = probs[:, 0, h, :]
                        else:
                            pool.wait_ge(summed, p.times(NSUM, kt - 1 if last else 2 * (kt - 2) + h + 1))
                            a = tot[:, h, :]
                        pool.tensor_tensor(tot[:, h, :], a, probs[:, kt % RING, h, :], ALU.add).then_inc(summed, 1)
                    if kt == 2 and behind == 2:
                        norm_o(p.step(-2), False)
                    if kt == 3 and last:
                        rstd_of(g0, 0, True)
                    if kt == 4 and last:
                        add_x(g0)
                    if kt == 5 and last:
                        norm_o(p.step(-1), False)
                        rstd_of(g0, 1, False)
                        rstd_of(g1, 0, True)
                if last:
                    add_x(g1)

            def rstd_of(g, k, shifted):
                s = g.parity
                mean, var = mean_var[k][s][:, :, 0], mean_var[k][s][:, :, 1]
                pool.wait_ge(norm_stats[k], g.times(1, 1))
                pool.tensor_tensor(rstd[k][s][:, :], var, eps_tile[k][:, :], ALU.add).then_inc(eps_added[k], 1)
                if shifted:
                    pool.tensor_tensor(shift[k][s][:, :], zeros[:, :], mean, ALU.subtract)\
                        .then_inc(mean_negated[k], 1)
                pool.wait_ge(eps_added[k], g.times(1, 1))
                pool.tensor_tensor(rstd[k][s][:, :], rstd[k][s][:, :], minus_half[:, :], ALU.pow)\
                    .then_inc(rstd_done[k], 1)
                if shifted:
                    pool.wait_ge(mean_negated[k], g.times(1, 1))
                    pool.wait_ge(rstd_done[k], g.times(1, 1))
                    pool.tensor_tensor(shift[k][s][:, :], shift[k][s][:, :], rstd[k][s][:, :], ALU.mult)\
                        .then_inc(shift_done[k], 1)

            def add_x(g):
                s = g.parity
                pool.wait_ge(t_ready, g.times(1, 1))
                tiles = split_tiles(t_buf[s])
                pool.tensor_tensor(tiles, tiles, gamma_all[:, :].unsqueeze(1).to_broadcast([128, GT, D]), ALU.mult)\
                    .then_inc(gamma_done, 1)
                pool.wait_ge(gamma_done, g.times(1, 1))
                pool.tensor_tensor(r1_buf[s], t_buf[s], x_tok[:, g.cols()], ALU.add).then_inc(r1_ready, 1)

            def group(g, has):
                if has(1):
                    rstd_of(g.step(1), 1, False)
                if has(2):
                    rstd_of(g.step(2), 0, True)
                    add_x(g.step(2))
                if has(-1):
                    rstd_of(g.step(-1), 2, True)

            pool.wait_ge(consts, 6)
            over_pairs(pool, pair, lambda p: pair(p, 2, True))
            over_groups(pool, group)

        @block.scalar
        def _(act):
            for k, w in enumerate((w_q, w_k, w_v)):
                act.dma_start(w_stage[k], w).then_inc(qkv_loaded[k], 16)
            for vec, all_ in ((b_proj, b_all), (ln_gamma, gamma_all), (ln_beta, beta_all)):
                act.dma_start(all_[:, :], vec.rearrange("(a n) -> a n", a=1).to_broadcast([128, D]))\
                   .then_inc(vec_loaded, 16)
            act.dma_start(wp_all[:, :, :], w_proj.rearrange("(j p) d -> p j d", p=128)).then_inc(wp_loaded, 16)
            for k, w in enumerate((w_gate, w_up)):
                act.dma_start(ffn_int[k].rearrange("p (j d) -> p j d", d=D), w.rearrange("(j p) d -> p j d", p=128))\
                   .then_inc(ffn_loaded, 16)
            act.dma_start(ffn_int[2], w_down).then_inc(ffn_loaded, 16)

            def split_w(k):
                act.wait_ge(qkv_loaded[k], 16)
                act.activation(w_split[:, :, 2 * k, :], w_stage[k].rearrange("p (j n) -> p j n", n=128),
                               ACT.Copy, scale=W_SCALE).then_inc(w_high, 1)

            def split_x(b):
                act.wait_ge(x_turned, b + 1)
                act.activation(x_split[:, b, 0, :], x_ps[b], ACT.Copy).then_inc(x_high, 1)

            def keep_q(n, first=False):
                act.wait_ge(q_proj, n.times(1, 1))
                if not first:
                    act.wait_ge(q_twin, n.times(4))
                act.activation(q_pair[0][:, :], side, ACT.Copy, scale=Q_SCALE).then_inc(q_high, 1)

            def keep_k(n, first=False):
                act.wait_ge(k_proj, n.times(1, 1))
                if not first:
                    before = n.step(-1)
                    act.wait_ge(k_twin, n.times(4))
                    act.wait_ge(halves_here[before.parity], before.second(64, 64))
                act.activation(k_pair[0][:, :], side, ACT.Copy, scale=1 / W_SCALE).then_inc(k_high, 1)

            def keep_v(n):
                act.wait_ge(v_proj, n.times(1, 1))
                act.activation(v_slot[n.parity][:, :, :], side.rearrange("p (t n) -> p t n", n=128), ACT.Copy,
                               scale=1 / W_SCALE).then_inc(v_kept, 1)

            def keep_max_rows(n, first=False):
                act.wait_ge(m_turned, n.times(1, 1))
                if not first:
                    before = n.step(-1)
                    act.wait_ge(m_here[before.parity], before.second(32, 32))
                act.activation(max_rows[:, :], side_bank[2][0:MAXJ // 2, 0:128], ACT.Copy).then_inc(m_rows, 1)

            def exp(p, kt, j, first, last):
                h, c = j // 2, j % 2
                act.wait_ge(scores, p.times(NSC, 4 * kt + j + 1))
                if c == 0 and (kt >= RING or not first):
                    act.wait_ge(weighed, p.times(KT, kt - RING + 1))
                if c == 0 and kt < RING and not first:
                    act.wait_ge(summed, p.times(NSUM, 2 * (kt - RING) + h + 1))
                elif c == 0 and kt >= RING and not last:
                    act.wait_ge(summed, p.times(NSUM, 2 * max(kt - RING - 1, 0) + h + 1))
                elif c == 0 and kt >= RING:
                    act.wait_ge((summed, summed_late)[h], (1 - h) * LAST * NSUM + max(kt - RING, 1))
                act.activation(probs[:, kt % RING, h, c * 512:(c + 1) * 512], score_bank[(4 * kt + j) % 3], ACT.Exp)\
                   .then_inc(exped, 1)

            def keep_o(q, first):
                act.wait_ge(weighed, q.times(KT, KT))
                if not first:
                    act.wait_ge(o_normed, q.times(1, -1))
                act.activation(o_raw[q.parity][:, :], o_ps, ACT.Copy).then_inc(o_kept, 1)

            def split_sum(q, h, first, last=False):
                if last:
                    act.wait_ge((summed, summed_late)[h], (1 - h) * LAST * NSUM + KT - 1)
                else:
                    act.wait_ge(summed, q.times(NSUM, NSUM - 1 + h))
                if not first:
                    act.wait_ge(sum_spread, q.times(1))
                act.activation(sum_split[:, 0, h, :], prob_sum[q.parity][:, h, :], ACT.Copy).then_inc(sum_high, 1)

            def keep_sum(q, first):
                act.wait_ge(sum_spread, q.times(1, 1))
                if not first:
                    act.wait_ge(inverted, q.times(KT, -KT))
                act.activation(row_sum[q.parity][:, :], side, ACT.Copy).then_inc(sum_kept, 1)

            start = Pair(act, 0, 0)
            split_w(0)
            split_x(0)
            split_w(1)
            split_w(2)
            keep_q(start, True)
            split_x(1)
            keep_k(start, True)
            keep_v(start)
            split_x(2)
            split_x(3)
            act.wait_ge(ffn_loaded, 48)
            for k in range(3):
                act.activation(ffn_f[k], ffn_int[k], ACT.Copy, scale=1.0 / 127.0).then_inc(ffn_cast, 1)
            for k, w_t in enumerate((wg_t, wu_t, wd_t)):
                act.wait_ge(ffn_turned, k + 1)
                act.activation(w_t[:, :, :], ffn_ps[k].rearrange("p (j n) -> p j n", n=128), ACT.Copy)\
                   .then_inc(ffn_kept, 1)
            keep_max_rows(start, True)

            def pair(p, behind, last):
                n, q = p.step(1), p.step(-1)
                first = behind == 0
                if behind:
                    split_sum(q, 0, behind == 1)
                if not last:
                    keep_q(n)
                if behind:
                    split_sum(q, 1, behind == 1)
                for kt in range(KT):
                    for j in range(4):
                        if (kt, j) == (1, 0) and not last:
                            keep_k(n)
                        if kt == 2 and j == 2 and behind:
                            keep_sum(q, behind == 1)
                        exp(p, kt, j, first, last)
                    if kt == 0 and behind:
                        keep_o(q, behind == 1)
                    if kt == 1 and not last:
                        keep_v(n)
                    if kt == 3 and last:
                        first_norm(Pair(act, 0, 0))
                if not last:
                    keep_max_rows(n)

            def apply(g, k, dst, src, done):
                s = g.parity
                act.wait_ge(shift_done[k], g.times(1, 1))
                for t in range(GT):
                    last = act.activation(dst[:, t, :], src[:, t, :], ACT.Identity, bias=shift[k][s][:, t:t + 1],
                                          scale=rstd[k][s][:, t:t + 1])
                last.then_inc(done, 1)

            def first_norm(g):
                if not g.early:
                    act.wait_ge(r1_ready, g.times(1, -1))
                apply(g, 0, split_tiles(t_buf[g.parity]), split_tiles(y_tok[:, g.cols()]), t_ready)

            def third_norm(g):
                s = g.parity
                act.wait_ge(out_free[s], g.second(16, 16))
                apply(g, 2, split_tiles(out_buf[s]), split_tiles(r2_buf[s]), out_ready)

            def turn_kept(g):
                act.wait_ge(x1_turned, g.times(1, 1))
                act.activation(x1_t[g.parity], turn_ps, ACT.Copy).then_inc(x1_t_kept, 1)

            def silu(g, j):
                act.wait_ge(gated, g.times(HB, j + 1))
                if not g.begin:
                    act.wait_ge(h_ready, g.times(HB, j + 1 - HB))
                act.activation(sil[:, j * GROUP:(j + 1) * GROUP], gate_ps[j], ACT.Silu).then_inc(silu_done, 1)

            def group(g, has):
                if has(0):
                    silu(g, 0)
                if has(2):
                    first_norm(g.step(2))
                if has(0):
                    silu(g, 1)
                if has(1):
                    turn_kept(g.step(1))
                if has(0):
                    silu(g, 2)
                if has(-1):
                    third_norm(g.step(-1))

            over_pairs(act, pair, lambda p: pair(p, 2, True))
            end = Pair(act, LAST // 2, LAST % 2)
            turn_kept(Pair(act, 0, 0))
            first_norm(Pair(act, 0, 1))
            keep_o(end, False)
            split_sum(end, 0, False, True)
            split_sum(end, 1, False, True)
            keep_sum(end, False)
            over_groups(act, group)

        @block.tensor
        def _(pe):
            pe.wait_ge(made, 4)

            def turn_x(b):
                pe.wait_ge(x_loaded[b], 16)
                if b >= 2:
                    pe.wait_ge(x_high, b - 1)
                    pe.wait_ge(x_low, b - 1)
                for t in range(KT):
                    cols = slice((b * KT + t) * D, (b * KT + t + 1) * D)
                    mm = pe.transpose(x_ps[b][:, t * 128:(t + 1) * 128], x_tok[:, cols], ident[:, :])
                mm.then_inc(x_turned, 1)

            def turn_ffn(k):
                for j in range(HB):
                    mm = pe.transpose(ffn_ps[k][:, j * 128:(j + 1) * 128], ffn_f[k][:, j * 128:(j + 1) * 128],
                                      ident[:, :])
                mm.then_inc(ffn_turned, 1)

            def project(w, x_hl, k, done):
                for t, (wp, xp) in enumerate(((2 * k, 1), (2 * k + 1, 0), (2 * k, 0))):
                    for c in range(2):
                        mm = pe.matmul(side_bank[c], w[:, wp, :], x_hl[:, xp, c * 512:(c + 1) * 512],
                                       start=t == 0, stop=t == 2)
                mm.then_inc(done, 1)

            def project_q(n):
                pe.wait_ge(w_here[n.parity], n.second(16, 16))
                pe.wait_ge(x_here, n.batch(16, 16))
                project(w_slot[n.parity], x_slot, 0, q_proj)

            def project_k(n):
                pe.wait_ge(q_high, n.times(1, 1))
                pe.wait_ge(q_low, n.times(1, 1))
                project(w_slot[n.parity], x_slot, 1, k_proj)

            def project_v(n):
                pe.wait_ge(k_high, n.times(1, 1))
                pe.wait_ge(k_low, n.times(1, 1))
                project_values(w_slot[n.parity], x_slot)

            def project_values(w, x_hl):
                for t in range(KT):
                    for i, (wp, xp) in enumerate(((4, 1), (5, 0), (4, 0))):
                        mm = pe.matmul(side[:, t * 128:(t + 1) * 128], x_hl[:, xp, t * 128:(t + 1) * 128],
                                       w[:, wp, :], start=i == 0, stop=i == 2)
                mm.then_inc(v_proj, 1)

            def max_tile(n, c, first=False):
                h, qt, half = c // (2 * KT), c // 2 % KT, c % 2
                banks = START_BANKS if first else MAX_BANKS
                if MAX_BANKS.index(2) == c and not first:
                    pe.wait_ge(m_rows, n.times(1))
                if c == 0:
                    pe.wait_ge(q_twin, n.times(4, 4))
                    pe.wait_ge(k_twin, n.times(4, 4))
                if banks[c] in banks[:c]:
                    pe.wait_ge(row_max, n.times(MAXJ, c - banks[:c][::-1].index(banks[c])))
                pe.matmul(side_bank[banks[c]], q_hh[n.parity][h][:, qt * 128:(qt + 1) * 128],
                          k_hl[n.parity][h][:, half * 512:(half + 1) * 512], start=True, stop=True)\
                  .then_inc(max_scores, 1)

            def turn_max(n):
                pe.wait_ge(m_joined, n.times(1, 1))
                pe.matmul(side_bank[2][0:MAXJ // 2, 0:128], max16[:, :], neg_ident[:, :], start=True, stop=True)\
                  .then_inc(m_turned, 1)

            def score_high(p, kt, j, first):
                k, h, c = 4 * kt + j, j // 2, j % 2
                if k >= 3:
                    pe.wait_ge(exped, p.times(NSC, k - 2))
                elif not first:
                    pe.wait_ge(exped, p.times(NSC, LAST_USE[k] + 1 - NSC))
                s = p.parity
                pe.matmul(score_bank[k % 3], k_hl[s][h][:, kt * 128:(kt + 1) * 128],
                          q_hh[s][h][:, c * 512:(c + 1) * 512], start=True, stop=False)

            def score_low(p, kt, j):
                k, h, c = 4 * kt + j, j // 2, j % 2
                s = p.parity
                if k == 0:
                    pe.wait_ge(m_here[s], p.second(32, 32))
                    pe.wait_ge(halves_here[s], p.second(64, 64))
                pe.matmul(score_bank[k % 3], k_h1[s][h][:, kt * 128:(kt + 1) * 128],
                          q_lm[s][h][:, c * 512:(c + 1) * 512], start=False, stop=True).then_inc(scores, 1)

            def weigh(p, kt, c, first):
                pe.wait_ge(exped, p.times(NSC, 4 * kt + c + 3))
                if kt == 0 and c == 0:
                    pe.wait_ge(v_kept, p.times(1, 1))
                    if not first:
                        pe.wait_ge(o_kept, p.times(1))
                for h in range(2):
                    mm = pe.matmul(o_ps[ROWS[h], c * 512:(c + 1) * 512], v_slot[p.parity][:, kt, ROWS[h]],
                                   probs[:, kt % RING, h, c * 512:(c + 1) * 512],
                                   start=kt == 0, stop=kt == KT - 1)
                if c == 1:
                    mm.then_inc(weighed, 1)

            def spread_sum(q):
                pe.wait_ge(sum_high, q.times(2, 2))
                pe.wait_ge(sum_low, q.times(2, 2))
                for c in range(2):
                    for part in (1, 0):
                        for h in range(2):
                            mm = pe.matmul(side[ROWS[h], c * 512:(c + 1) * 512], ones64[:, :],
                                           sum_split[:, part, h, c * 512:(c + 1) * 512],
                                           start=part == 1, stop=part == 0)
                mm.then_inc(sum_spread, 1)

            def project_o(q):
                pe.wait_ge(o_normed, q.times(1, 1))
                pe.wait_ge(wp_here[q.parity], q.second(16, 16))
                for t in range(KT):
                    mm = pe.matmul(side[:, t * D:(t + 1) * D], o_norm[:, t * 128:(t + 1) * 128],
                                   wp_slot[q.parity][:, :], start=True, stop=True)
                mm.then_inc(projected, 1)

            start = Pair(pe, 0, 0)
            turn_x(0)
            w0, x0 = w_split[:, 0, :, :], x_split[:, 0, :, :]
            pe.wait_ge(w_high, 1)
            pe.wait_ge(w_low, 1)
            pe.wait_ge(x_high, 1)
            pe.wait_ge(x_low, 1)
            project(w0, x0, 0, q_proj)
            turn_x(1)
            pe.wait_ge(w_high, 2)
            pe.wait_ge(w_low, 2)
            pe.wait_ge(q_high, 1)
            pe.wait_ge(q_low, 1)
            project(w0, x0, 1, k_proj)
            turn_x(2)
            pe.wait_ge(w_high, 3)
            pe.wait_ge(w_low, 3)
            pe.wait_ge(k_high, 1)
            pe.wait_ge(k_low, 1)
            project_values(w0, x0)
            turn_x(3)
            pe.wait_ge(v_kept, 1)
            for c in range(MAXJ):
                max_tile(start, c, True)
            pe.wait_ge(ffn_cast, 3)
            pe.wait_ge(x_high, B)
            pe.wait_ge(x_low, B)
            for k in range(3):
                turn_ffn(k)
            turn_max(start)
            pe.wait_ge(ffn_kept, 3)
            pe.wait_ge(padded, 8)
            pe.wait_ge(consts, 1)
            pe.wait_ge(q_low, 1)

            def pair(p, behind, last):
                n, q, r = p.step(1), p.step(-1), p.step(-2)
                first = behind == 0
                for j in (2, 0, 1):
                    score_high(p, 0, j, first)
                if not last:
                    project_q(n)
                if behind:
                    weigh(q, KT - 1, 0, behind == 1)
                    weigh(q, KT - 1, 1, behind == 1)
                for j in range(3):
                    score_low(p, 0, j)
                score_high(p, 0, 3, first)
                score_low(p, 0, 3)
                if not last:
                    project_k(n)
                c = 0
                for kt in range(1, KT):
                    for point, work in enumerate(POINTS):
                        at = (kt, point)
                        if work in range(4):
                            score_high(p, kt, work, first)
                            score_low(p, kt, work)
                        else:
                            weigh(p, kt - 1, int(work[-1]), first)
                        for _ in () if last else MAX_TILES.get(at, ()):
                            if behind and c == AFTER_SPREAD:
                                pe.wait_ge(sum_kept, q.times(1, 1))
                            if not behind and c == AFTER_SPREAD:
                                pe.wait_ge(v_kept, n.times(1, 1))
                            if behind == 2 and c == AFTER_O:
                                pe.wait_ge(y_added, r.times(1, 1))
                            max_tile(n, c)
                            c += 1
                        if at == V_AT and not last:
                            project_v(n)
                        if at == SPREAD_AT and behind:
                            if not last:
                                pe.wait_ge(v_kept, n.times(1, 1))
                            spread_sum(q)
                        if at == O_AT and behind == 2:
                            if last:
                                pe.wait_ge(sum_kept, q.times(1, 1))
                            else:
                                pe.wait_ge(row_max, n.times(MAXJ, BEFORE_O + 1))
                            project_o(r)
                        if at == LAST_O_AT and last:
                            pe.wait_ge(y_added, r.times(1, 1))
                            project_o(q)
                        if at == TURN_AT and not last:
                            turn_max(n)

            over_pairs(pe, pair, lambda p: pair(p, 2, True))
            end = Pair(pe, LAST // 2, LAST % 2)
            weigh(end, KT - 1, 0, False)
            weigh(end, KT - 1, 1, False)

            def project_end(half):
                for t in range(KT // 2):
                    part = half * (KT // 2) + t
                    pe.wait_ge(end_normed, part + 1)
                    mm = pe.matmul(down_ps[:, t * D:(t + 1) * D], o_norm[:, part * 128:(part + 1) * 128],
                                   wp_slot[end.parity][:, :], start=True, stop=True)
                mm.then_inc(end_projected, 1)

            def turn(g):
                pe.wait_ge(x1_ready, g.times(1, 1))
                if not g.begin:
                    pe.wait_ge(x1_t_kept, g.times(1))
                for t in range(GT):
                    mm = pe.transpose(turn_ps[:, t * 128:(t + 1) * 128], x1_buf[g.parity][:, t * D:(t + 1) * D],
                                      ident[:, :])
                mm.then_inc(x1_turned, 1)

            def gate_up(g, j):
                if j == 0:
                    pe.wait_ge(x1_t_kept, g.times(1, 1))
                if not g.begin:
                    pe.wait_ge(h_ready, g.times(HB, j + 1 - HB))
                for w_t, dst in ((wg_t, gate_ps), (wu_t, up_ps)):
                    mm = pe.matmul(dst[j], w_t[:, j, :], x1_t[g.parity], start=True, stop=True)
                mm.then_inc(gated, 1)

            def down(g):
                pe.wait_ge(h_ready, g.times(HB, HB))
                if not g.begin:
                    pe.wait_ge(r2_ready, g.times(1))
                for t in range(GT):
                    for j in range(HB):
                        mm = pe.matmul(down_ps[:, t * D:(t + 1) * D],
                                       h_buf[g.parity][:, j * GROUP + t * 128:j * GROUP + (t + 1) * 128],
                                       wd_t[:, j, :], start=j == 0, stop=j == HB - 1)
                mm.then_inc(downed, 1)

            def group(g, has):
                if has(0):
                    gate_up(g, 0)
                if g.number == 0:
                    pe.wait_ge(y_added, LAST)
                    spread_sum(end)
                    pe.wait_ge(o_kept, PAIRS)
                if g.number == 1:
                    pe.wait_ge(end_added, 1)
                    project_end(1)
                    pe.wait_ge(end_added, 2)
                if has(-1):
                    down(g.step(-1))
                if has(0):
                    gate_up(g, 1)
                if has(1):
                    turn(g.step(1))
                if g.number == 0:
                    pe.wait_ge(sum_kept, PAIRS)
                if has(0):
                    gate_up(g, 2)
                if g.number == 0:
                    pe.wait_ge(wp_here[end.parity], end.second(16, 16))
                    project_end(0)

            turn(Pair(pe, 0, 0))
            over_groups(pe, group)

        @block.vector
        def _(dve):
            for s in range(2):
                for h in range(2):
                    other = ROWS[1 - h]
                    dve.memset(k_h1[s][h][other, :], 1.0).then_inc(padded, 1)
                    dve.memset(q_lm[s][h][other, :], 0.0).then_inc(padded, 1)
            def split_w(k):
                dve.wait_ge(w_high, k + 1)
                dve.scalar_tensor_tensor(out=w_split[:, :, 2 * k + 1, :],
                                         in0=w_stage[k].rearrange("p (j n) -> p j n", n=128), scalar=W_SCALE,
                                         in1=w_split[:, :, 2 * k, :], op0=ALU.mult, op1=ALU.subtract)\
                   .then_inc(w_low, 1)

            def split_x(b):
                dve.wait_ge(x_high, b + 1)
                dve.tensor_tensor(x_split[:, b, 1, :], x_ps[b], x_split[:, b, 0, :], ALU.subtract).then_inc(x_low, 1)

            def part_q(n, first=False):
                s, before = n.parity, n.step(-1)
                dve.wait_ge(q_proj, n.times(1, 1))
                dve.wait_ge(q_high, n.times(1, 1))
                if not first:
                    dve.wait_ge(halves_here[before.parity], before.second(64, 64))
                dve.scalar_tensor_tensor(out=q_pair[1][:, :], in0=side, scalar=Q_SCALE, in1=q_pair[0][:, :],
                                         op0=ALU.mult, op1=ALU.subtract).then_inc(q_low, 1)
                for h in range(2):
                    for half in ROWS:
                        dve.tensor_copy(q_hh[s][h][half, :], q_pair[0][ROWS[h], :]).then_inc(q_twin, 1)

            def part_k(n, first=False):
                s = n.parity
                dve.wait_ge(k_proj, n.times(1, 1))
                dve.wait_ge(k_high, n.times(1, 1))
                if not first:
                    dve.wait_ge(k_twin, n.times(4))
                dve.scalar_tensor_tensor(out=k_pair[1][:, :], in0=side, scalar=1 / W_SCALE, in1=k_pair[0][:, :],
                                         op0=ALU.mult, op1=ALU.subtract).then_inc(k_low, 1)
                for h in range(2):
                    dve.tensor_copy(k_hl[s][h][ROWS[h], :], k_pair[0][ROWS[h], :]).then_inc(k_twin, 1)
                dve.wait_ge(k_low, n.times(1, 1))
                for h in range(2):
                    dve.tensor_copy(k_hl[s][h][ROWS[1 - h], :], k_pair[1][ROWS[h], :]).then_inc(k_twin, 1)

            def max_tile(n, c, banks=MAX_BANKS):
                dve.wait_ge(max_scores, n.times(MAXJ, c + 1))
                dve.tensor_reduce(tile_max[:, c // 2, c % 2:c % 2 + 1], side_bank[banks[c]], AX_X, ALU.max)\
                   .then_inc(row_max, 1)

            def join_max(n, first=False):
                dve.wait_ge(row_max, n.times(MAXJ, MAXJ))
                if not first:
                    dve.wait_ge(m_turned, n.times(1))
                dve.tensor_tensor(max16[:, :], tile_max[:, :, 0], tile_max[:, :, 1], ALU.max).then_inc(m_joined, 1)

            def invert(q, part, first=False):
                dve.wait_ge(sum_kept, q.times(1, 1))
                if part == 0 and not first:
                    dve.wait_ge(o_normed, q.times(1))
                cols = slice(part * (S // KT), (part + 1) * (S // KT))
                dve.reciprocal(row_inv[:, cols], row_sum[q.parity][:, cols]).then_inc(inverted, 1)

            def split_sum(q, h):
                dve.wait_ge(sum_high, q.times(2, h + 1))
                dve.tensor_tensor(sum_split[:, 1, h, :], prob_sum[q.parity][:, h, :], sum_split[:, 0, h, :],
                                  ALU.subtract).then_inc(sum_low, 1)

            def add_y(q):
                dve.wait_ge(projected, q.times(1, 1))
                y = y_tok[:, q.batch_cols()]
                dve.tensor_tensor(y, side, y, ALU.add).then_inc(y_added, 1)

            start = Pair(dve, 0, 0)
            split_w(0)
            split_x(0)
            split_w(1)
            split_w(2)
            part_q(start, True)
            split_x(1)
            part_k(start, True)
            for c in range(MAXJ):
                max_tile(start, c, START_BANKS)
                if c in (3, 7):
                    split_x(2 + c // 4)
            join_max(start, True)
            dve.wait_ge(y_begun, 2 * B)

            def pair(p, behind, last):
                n, r = p.step(1), p.step(-2)
                for part in range(3):
                    if behind == 2:
                        invert(r, part, False)
                if behind:
                    split_sum(p.step(-1), 0)
                part_q(n)
                if behind:
                    split_sum(p.step(-1), 1)
                if behind == 2:
                    invert(r, 3, False)
                part_k(n)
                for c in range(MAXJ):
                    if c == O_TILES and behind == 2:
                        add_y(r)
                    max_tile(n, c)
                    if behind == 2 and c < 4:
                        invert(r, 4 + c, False)
                join_max(n)

            def last_pair(p):
                q, r = p.step(-1), p.step(-2)
                g0, g1 = Pair(dve, 0, 0), Pair(dve, 0, 1)
                for part in range(KT):
                    invert(r, part)
                split_sum(q, 0)
                split_sum(q, 1)
                inverts = {3: (0, 1, 2), 4: (3, 4, 5), 5: (6, 7)}
                tot = prob_sum[p.parity][:, 1, :]
                for kt in range(1, KT):
                    dve.wait_ge(exped, p.times(NSC, 4 * kt + 4))
                    if kt == 1:
                        dve.wait_ge(sum_spread, p.times(1, -1))
                        a = probs[:, 0, 1, :]
                    else:
                        dve.wait_ge(summed_late, kt - 1)
                        a = tot
                    dve.tensor_tensor(tot, a, probs[:, kt % RING, 1, :], ALU.add).then_inc(summed_late, 1)
                    for part in inverts.get(kt, ()):
                        invert(q, part)
                    if kt == 2:
                        dve.wait_ge(y_added, PAIRS - PB)
                        first_norm(g0)
                    if kt == 5:
                        add_y(r)
                        second_stats(g0)
                        first_norm(g1)
                    if kt == 6:
                        second_apply(g0)
                add_y(q)

            def norm_end(*parts_now):
                for part in parts_now:
                    dve.wait_ge(sum_kept, PAIRS)
                    dve.wait_ge(o_normed, LAST)
                    cols = slice(part * (S // KT), (part + 1) * (S // KT))
                    dve.reciprocal(row_inv[:, cols], row_sum[LAST % 2][:, cols]).then_inc(inverted, 1)
                for part in parts_now:
                    dve.wait_ge(inverted, LAST * KT + part + 1)
                    dve.wait_ge(o_kept, PAIRS)
                    dve.wait_ge(projected, LAST)
                    cols = slice(part * (S // KT), (part + 1) * (S // KT))
                    dve.tensor_tensor(o_norm[:, cols], o_raw[LAST % 2][:, cols], row_inv[:, cols], ALU.mult)\
                       .then_inc(end_normed, 1)

            def add_end(half):
                dve.wait_ge(end_projected, half + 1)
                y = y_tok[:, (2 * B - 2 + half) * (S // 2):(2 * B - 1 + half) * (S // 2)]
                dve.tensor_tensor(y, down_ps, y, ALU.add).then_inc(end_added, 1)

            def stats_of(g, k, tiles):
                s = g.parity
                for t in range(GT):
                    dve.bn_stats(parts[k][s][:, t, :], tiles[:, t, :]).then_inc(norm_parts[k], 1)
                for t in range(GT):
                    if t == 0:
                        dve.wait_ge(norm_parts[k], g.times(GT, GT))
                        dve.sem_inc(parts_seen, 1)
                    last = dve.bn_aggr(mean_var[k][s][:, t, :], parts[k][s][:, t, :])
                last.then_inc(norm_stats[k], 1)

            def first_norm(g):
                stats_of(g, 0, split_tiles(y_tok[:, g.cols()]))

            def second_stats(g):
                dve.wait_ge(r1_ready, g.times(1, 1))
                stats_of(g, 1, split_tiles(r1_buf[g.parity]))

            def second_apply(g):
                s = g.parity
                dve.wait_ge(rstd_done[1], g.times(1, 1))
                if not g.early:
                    dve.wait_ge(x1_turned, g.times(1, -1))
                    dve.wait_ge(r2_ready, g.times(1, -1))
                for t in range(GT):
                    cols = slice(t * D, (t + 1) * D)
                    last = dve.tensor_scalar(x1_buf[s][:, cols], r1_buf[s][:, cols], mean_var[1][s][:, t, 0:1],
                                             rstd[1][s][:, t:t + 1], ALU.subtract, ALU.mult)
                last.then_inc(x1_ready, 1)

            def hidden(g, j):
                dve.wait_ge(silu_done, g.times(HB, j + 1))
                if not g.early:
                    dve.wait_ge(downed, g.times(1, -1))
                cols = slice(j * GROUP, (j + 1) * GROUP)
                dve.tensor_tensor(h_buf[g.parity][:, cols], up_ps[j], sil[:, cols], ALU.mult).then_inc(h_ready, 1)

            def add_x1(g):
                s = g.parity
                dve.wait_ge(downed, g.times(1, 1))
                if not g.early:
                    dve.wait_ge(out_ready, g.times(1, -1))
                dve.tensor_tensor(r2_buf[s], down_ps, x1_buf[s], ALU.add).then_inc(r2_ready, 1)

            def third_stats(g):
                dve.wait_ge(r2_ready, g.times(1, 1))
                stats_of(g, 2, split_tiles(r2_buf[g.parity]))

            def group(g, has):
                if g.number == 0:
                    end = Pair(dve, LAST // 2, LAST % 2)
                    for h in range(2):
                        split_sum(end, h)
                if g.number == 1:
                    add_end(1)
                if has(1):
                    second_stats(g.step(1))
                if has(2):
                    first_norm(g.step(2))
                if g.number == 0:
                    norm_end(0, 1)
                    second_apply(g.step(1))
                if has(0):
                    hidden(g, 0)
                if g.number == 0:
                    norm_end(2, 3)
                if has(-1):
                    add_x1(g.step(-1))
                if has(1) and g.number != 0:
                    second_apply(g.step(1))
                if has(-1):
                    third_stats(g.step(-1))
                if has(0):
                    hidden(g, 1)
                if g.number == 0:
                    norm_end(4, 5)
                    add_end(0)
                    norm_end(6, 7)
                if has(0):
                    hidden(g, 2)
                if g.number == 1:
                    dve.wait_ge(end_added, 2)

            over_pairs(dve, pair, last_pair)
            over_groups(dve, group)


_INS = ['L0_attn_x', 'L0_attn_w_q', 'L0_attn_w_k', 'L0_attn_w_v', 'L0_attn_w_proj', 'L0_attn_b_proj',
        'L0_attn_ln_gamma', 'L0_attn_ln_beta', 'L0_ffn_w_gate', 'L0_ffn_w_up', 'L0_ffn_w_down']
_OUTS = [((4, 1024, 128), 'float32')]


def kernel(**inputs):
    import numpy as _np
    import concourse.bacc as _bacc
    from concourse import mybir as _mybir
    from concourse.bass_utils import run_bass_kernel_spmd as _run

    nc = _bacc.Bacc("TRN2", target_bir_lowering=False, num_devices=1)
    arrays, args = {}, []
    for name in _INS:
        a = _np.ascontiguousarray(inputs[name])
        arrays[f"in_{name}_dram"] = a
        args.append(nc.dram_tensor(f"in_{name}_dram", a.shape, _mybir.dt.from_np(a.dtype), kind="ExternalInput").ap())
    for i, (shape, dtype) in enumerate(_OUTS):
        dt = _mybir.dt.from_np(_np.dtype(dtype))
        args.append(nc.dram_tensor(f"out_{i}_dram", shape, dt, kind="ExternalOutput").ap())
    attention_ffn_program(nc, *args)
    r = _run(nc, [arrays], core_ids=[0])
    return r.results[0]["out_0_dram"]
```
